# Optimizing a Trainium2 kernel written in Bass

```python
import numpy as np
import jax
import jax.numpy as jnp

def _softmax(x, axis=-1):
    return jax.nn.softmax(x, axis=axis)

def _gelu(x):
    return jax.nn.gelu(x, approximate=True)

def _silu(x):
    return jax.nn.silu(x)

def _sigmoid(x):
    return jax.nn.sigmoid(x)

def _layernorm(x, axis=-1, eps=1e-05):
    m = jnp.mean(x, axis=axis, keepdims=True)
    v = jnp.var(x, axis=axis, keepdims=True)
    return (x - m) / jnp.sqrt(v + eps)

def _scatter_add(tgt, idx, src, axis=0):
    return tgt.at[idx].add(src)

def _segment_sum(src, seg, n):
    return jax.ops.segment_sum(src, seg, n)
kernel_name = 'mk_adj_resnorm_d4_adj_r2_aa1e63'

def setup_inputs(seed: int=0):
    np.random.seed(seed)
    _w = jnp.asarray

    def _rec_inputs():
        import jax
        import jax.numpy as jnp
        _gk = jax.random.key(seed)
        x = -0.0002928 + 1 * jax.random.normal(jax.random.fold_in(_gk, 1), (2048, 256), jnp.float32)
        _w = (1.0 + jnp.arange(2048, dtype=jnp.float32)) ** (-0.5)
        _w = _w / _w.mean()
        _pij = jnp.clip(0.000976562 * _w[:, None] * _w[None, :], 0.0, 1.0)
        _a = jax.random.uniform(jax.random.fold_in(_gk, 2), (2048, 2048)) < _pij
        _af = _a.astype(jnp.float32)
        adj = _af
        return (x, adj)
    x, adj = _rec_inputs()

    def _L0_gnn_setup():
        import jax, jax.numpy as jnp
        import numpy as np
        N = 4096
        D_IN = 256
        HEADS = 8
        DPH = 256 // HEADS
        EDGE_P = 0.01
        key = jax.random.key(seed)
        k1, k2, k3 = jax.random.split(key, 3)
        H = jax.random.normal(k1, (N, D_IN), dtype=jnp.float32)
        adj = (jax.random.uniform(k2, (N, N)) < EDGE_P).astype(jnp.float32)
        limit = float(np.sqrt(6.0 / (D_IN + DPH)))
        W = jax.random.uniform(k3, (HEADS, D_IN, DPH), jnp.float32, -limit, limit)
        b = jnp.zeros((HEADS, DPH), jnp.float32)
        return {'H': H, 'adj': adj, 'W': W, 'b': b}
    _L0_gnn_all = _L0_gnn_setup()
    _L0_gnn_in = {k: v for k, v in _L0_gnn_all.items() if k in ('W', 'b')}
    del _L0_gnn_all

    def _L1_gnn_setup():
        import jax, jax.numpy as jnp
        import numpy as np
        N_HEADS = 4
        N_HIDDEN = 256
        SLOPE = 0.01
        NEG = -1000000000.0
        key = jax.random.key(seed)
        k1, k2, k3, k4 = jax.random.split(key, 4)
        N, F_IN = (4096, 256)
        h = jax.random.normal(k1, (N, F_IN), dtype=jnp.float32)
        W = jax.random.normal(k2, (F_IN, N_HIDDEN * N_HEADS), dtype=jnp.float32) * 0.05
        a = jax.random.normal(k3, (N_HEADS, 2 * N_HIDDEN, 1), dtype=jnp.float32) * 0.05
        adj_mat = jnp.where(jax.random.uniform(k4, (N, N)) < 0.01, 0.0, NEG).astype(jnp.float32)
        return {'h': h, 'adj_mat': adj_mat, 'W': W, 'a': a}
    _L1_gnn_all = _L1_gnn_setup()
    _L1_gnn_in = {k: v for k, v in _L1_gnn_all.items() if k in ('W', 'a')}
    del _L1_gnn_all

    def _L2_gnn_setup():
        import jax, jax.numpy as jnp
        import numpy as np
        N = 4096
        D = 256
        H = 256

        def _graph_conv(feats, adj, W, b):
            agg = adj @ feats
            cat = jnp.concatenate([feats, agg], axis=-1)
            return jax.nn.relu(jnp.einsum('nd,df->nf', cat, W) + b)
        key = jax.random.key(seed)
        k1, k2, k3, k4 = jax.random.split(key, 4)
        x = jax.random.normal(k1, (N, D), dtype=jnp.float32)
        adj = jax.random.uniform(k2, (N, N), dtype=jnp.float32)
        adj = adj / jnp.sum(adj, axis=-1, keepdims=True)
        lim1 = float(np.sqrt(6.0 / (2 * D + H)))
        lim2 = float(np.sqrt(6.0 / (2 * H + H)))
        W1 = jax.random.uniform(k3, (2 * D, H), dtype=jnp.float32, minval=-lim1, maxval=lim1)
        W2 = jax.random.uniform(k4, (2 * H, H), dtype=jnp.float32, minval=-lim2, maxval=lim2)
        b1 = jnp.zeros((H,), dtype=jnp.float32)
        b2 = jnp.zeros((H,), dtype=jnp.float32)
        return {'x': x, 'adj': adj, 'W1': W1, 'b1': b1, 'W2': W2, 'b2': b2}
    _L2_gnn_all = _L2_gnn_setup()
    _L2_gnn_in = {k: v for k, v in _L2_gnn_all.items() if k in ('W1', 'b1', 'W2', 'b2')}
    del _L2_gnn_all

    def _L3_gnn_setup():
        import jax, jax.numpy as jnp
        import numpy as np
        N = 4096
        IN_F = 256
        OUT_F = 256
        key = jax.random.key(seed)
        k1, k2, k3 = jax.random.split(key, 3)
        x = jax.random.normal(k1, (N, IN_F), dtype=jnp.float32)
        adj = jax.random.uniform(k2, (N, N), dtype=jnp.float32)
        W = jax.random.normal(k3, (IN_F, OUT_F), dtype=jnp.float32) * 0.1
        return {'x': x, 'adj': adj, 'W': W}
    _L3_gnn_all = _L3_gnn_setup()
    _L3_gnn_in = {k: v for k, v in _L3_gnn_all.items() if k in ('W',)}
    del _L3_gnn_all
    return {'x': x, 'adj': adj, 'L0_gnn_W': _L0_gnn_in['W'], 'L0_gnn_b': _L0_gnn_in['b'], 'L1_gnn_W': _L1_gnn_in['W'], 'L1_gnn_a': _L1_gnn_in['a'], 'L2_gnn_W1': _L2_gnn_in['W1'], 'L2_gnn_b1': _L2_gnn_in['b1'], 'L2_gnn_W2': _L2_gnn_in['W2'], 'L2_gnn_b2': _L2_gnn_in['b2'], 'L3_gnn_W': _L3_gnn_in['W']}

def reference(x, adj, L0_gnn_W, L0_gnn_b, L1_gnn_W, L1_gnn_a, L2_gnn_W1, L2_gnn_b1, L2_gnn_W2, L2_gnn_b2, L3_gnn_W):
    import jax
    import jax.numpy as jnp

    def _L0_gnn_ref(H, adj, W, b):
        import jax, jax.numpy as jnp
        import numpy as np
        N = 4096
        D_IN = 256
        HEADS = 8
        DPH = 256 // HEADS
        EDGE_P = 0.01
        H_ = jnp.einsum('nd,hde->hne', H, W)
        out = jnp.einsum('nm,hme->hne', adj, H_) + b[:, None, :]
        return jnp.transpose(out, (1, 0, 2)).reshape(H.shape[0], HEADS * DPH)

    def _L1_gnn_ref(h, adj_mat, W, a):
        import jax, jax.numpy as jnp
        import numpy as np
        N_HEADS = 4
        N_HIDDEN = 256
        SLOPE = 0.01
        NEG = -1000000000.0
        N = h.shape[0]
        ht = (h @ W).reshape(N, N_HEADS, N_HIDDEN).transpose(1, 0, 2)
        a_src = a[:, :N_HIDDEN, 0]
        a_dst = a[:, N_HIDDEN:, 0]
        src = jnp.einsum('hnd,hd->hn', ht, a_src)
        dst = jnp.einsum('hnd,hd->hn', ht, a_dst)
        e = jax.nn.leaky_relu(src[:, :, None] + dst[:, None, :], SLOPE) + adj_mat[None]
        att = jax.nn.softmax(e, axis=-1)
        h_prime = jnp.einsum('hij,hjd->hid', att, ht)
        return h_prime.mean(axis=0)

    def _L2_gnn_ref(x, adj, W1, b1, W2, b2):
        import jax, jax.numpy as jnp
        import numpy as np
        N = 4096
        D = 256
        H = 256

        def _graph_conv(feats, adj, W, b):
            agg = adj @ feats
            cat = jnp.concatenate([feats, agg], axis=-1)
            return jax.nn.relu(jnp.einsum('nd,df->nf', cat, W) + b)
        h = _graph_conv(x, adj, W1, b1)
        out = jax.nn.relu(_graph_conv(h, adj, W2, b2) + h)
        return out

    def _L3_gnn_ref(x, adj, W):
        import jax, jax.numpy as jnp
        import numpy as np
        N = 4096
        IN_F = 256
        OUT_F = 256
        n = adj.shape[0]
        adj_hat = adj + jnp.eye(n, dtype=adj.dtype)
        degree = adj_hat.sum(axis=1)
        d_inv_sqrt = degree ** (-0.5)
        adj_norm = d_inv_sqrt[:, None] * adj_hat * d_inv_sqrt[None, :]
        return jax.nn.relu(adj_norm @ x @ W)
    x = _layernorm(x + _L0_gnn_ref(x, adj, L0_gnn_W, L0_gnn_b), axis=-1)
    x = _layernorm(x + _L1_gnn_ref(x, adj, L1_gnn_W, L1_gnn_a), axis=-1)
    x = _layernorm(x + _L2_gnn_ref(x, adj, L2_gnn_W1, L2_gnn_b1, L2_gnn_W2, L2_gnn_b2), axis=-1)
    x = _layernorm(x + _L3_gnn_ref(x, adj, L3_gnn_W), axis=-1)
    return x

_drawn_inputs = setup_inputs


def setup_inputs(seed=0):
    import zlib

    import numpy as np

    out = dict(_drawn_inputs(seed))
    spreads = {'L0_gnn_b': (0.0, 0.1), 'L2_gnn_b1': (0.0, 0.1), 'L2_gnn_b2': (0.0, 0.1)}
    factors = {}
    for name, (base, spread) in spreads.items():
        noise = np.random.default_rng([zlib.crc32(name.encode()), seed]).standard_normal(out[name].shape)
        drawn = base * np.exp(spread * noise) if base else spread * noise
        out[name] = jnp.asarray(drawn.astype(out[name].dtype))
    for name, factor in factors.items():
        out[name] = (out[name] * factor).astype(out[name].dtype)
    return out
```

```python
import math
from contextlib import ExitStack

import concourse.bass as bass
from concourse import mybir


def graph_stack(nc, x_in, adj_in, w0_in, b0_in, w1_in, a_in, w2a_in, b1_in, w2b_in, b2_in, w3_in, out):
    F32, F16, BF16 = mybir.dt.float32, mybir.dt.float16, mybir.dt.bfloat16
    ALU, ACT, AX = mybir.AluOpType, mybir.ActivationFunctionType, mybir.AxisListType

    P = 128
    N, D = x_in.shape
    T = N // P
    H, A2 = a_in.shape[0], a_in.shape[1]
    K2 = D // P
    KI = 2 * K2 * P
    R = 4
    CH = R * P
    PAIRS = (N // CH) * (H // 2)
    STEPS = PAIRS * T
    PW = D + 2
    WS = 64.0
    LCAP = 6 * math.log(2.0)
    SLOPE = 0.01
    EPS = 1e-5
    NL = 16
    LW = N // (NL // 2)
    JH = T // 2

    ctx = ExitStack()
    with ctx:
        def sb(name, shape, dt):
            return ctx.enter_context(nc.sbuf_tensor(name, shape, dt))

        def sem(name):
            return ctx.enter_context(nc.semaphore(name))

        adj = sb("adj", [P, T, N], BF16)
        x = sb("x", [P, T, D], F32)
        arena = sb("arena", [P, 2 * T * H * PW // 2], F32)
        w0 = sb("w0", [P, 2, K2, D], F16)
        w1 = sb("w1", [P, 2, K2, H * D], F16)
        w2a = sb("w2a", [P, 2, K2, 2 * D], F16)
        w2b = sb("w2b", [P, 2, K2, 2 * D], F16)
        w3 = sb("w3", [P, 2, K2, D], F16)
        rho = sb("rho", [P, 2, 2, CH], F32)
        ring_e = sb("ring_e", [P, 2, CH], F32)
        ring_a = sb("ring_a", [P, 2, 2, CH], F32)
        ring_hl = sb("ring_hl", [P, 4, 2, 2, CH], F16)
        ident = sb("ident", [P, P], F16)
        stat = sb("stat", [P, R, 6], F32)
        mv = sb("mv", [P, R, 2], F32)
        veps = sb("veps", [P, R], F32)
        rstd = sb("rstd", [P, R], F32)
        epsv = sb("epsv", [P, 1], F32)
        held = sb("held", [P, 1], F32)
        total = sb("total", [P, R, D], F32)
        b12 = w0[:, :, :, :].rearrange("p a k f -> p (a k f)").bitcast(F32).rearrange("p (a f) -> p a f", a=2)
        bias0 = total[:, R - 1, :]
        neghalf = sb("neghalf", [P, T], F32)
        deg = sb("deg", [P, T], F32)
        degp = sb("degp", [P, T], F32)
        dis = sb("dis", [P, T], F32)
        disw = sb("disw", [P, T], F32)
        wa = sb("wa", [P, K2, 2, H], F32)
        was = sb("was", [P, 2, K2, 2, H], F16)
        dall = sb("dall", [P, T, H], F32)
        dmx = sb("dmx", [P, H], F32)
        dmb = sb("dmb", [P, H], F32)
        bias_g = sb("bias_g", [P, H], F32)
        bias_b = sb("bias_b", [P, H], F32)
        gam = sb("gam", [P, H, T], F32)
        bet = sb("bet", [P, H, T], F32)
        betw = sb("betw", [P, H, T], F32)
        bet4 = sb("bet4", [P, H, T], F32)
        rden = sb("rden", [P, 2 * R], F32)
        ps = ctx.enter_context(nc.psum_tensor("ps", [P, 8, 512], F32))
        s_dram = nc.dram_tensor("s_scratch", [H, N], F32, kind="Internal").ap()

        def part(base, words, dt, text, **kw):
            v = base[:, words[0]:words[1]]
            if dt is not F32:
                v = v.bitcast(dt)
            return v.rearrange(text, **kw) if text else v

        PSET = T * 2 * PW // 2
        pset = [part(arena, (s * PSET, (s + 1) * PSET), F16, "p (t q f) -> p t q f", t=T, q=2) for s in range(2)]
        own = part(arena, (2 * PSET, 2 * PSET + T * D), F32, "p (t f) -> p t f", t=T)
        hid = part(arena, (2 * PSET + T * D, 2 * PSET + 2 * T * D), F32, "p (t f) -> p t f", t=T)
        STAGES = 4
        SW = JH * LW
        stage = part(arena, (PSET, PSET + STAGES * SW), F32, "p (s w) -> p s w", s=STAGES)
        w1f = part(arena, (PSET + STAGES * SW, PSET + STAGES * SW + K2 * H * D), F32, "p (k h f) -> p k h f", k=K2, h=H)
        o = PSET + STAGES * SW + K2 * H * D
        abc = part(arena, (o, o + H * A2), F32, "p (h s f) -> p h s f", h=H, s=2)
        VW = T * H * PW // 2
        val = [part(arena, (s * VW, (s + 1) * VW), F16, "p (t h f) -> p t h f", t=T, h=H) for s in range(2)]
        a_flat = ring_a[:, :, :, :].rearrange("p a b c -> p (a b c)")
        xs = part(a_flat, (0, R * D), F16, "p (s q f) -> p s q f", s=R, q=2)
        w0f = part(a_flat, (R * D, R * D + K2 * D), F32, "p (k f) -> p k f", k=K2)
        w3f = part(a_flat, (R * D + K2 * D, R * D + 2 * K2 * D), F32, "p (k f) -> p k f", k=K2)
        r_flat = rho[:, :, :, :].rearrange("p a b c -> p (a b c)")
        w2af = part(r_flat, (0, 4 * D), F32, "p (s k f) -> p k s f", s=2, k=K2)
        w2bf = part(r_flat, (4 * D, 8 * D), F32, "p (s k f) -> p k s f", s=2, k=K2)
        srow = r_flat[0:H, :]
        prod = ring_e[:, :, :].rearrange("p a (h f) -> p (a h) f", f=D)
        xt = ring_hl[:, :, :, :, :].rearrange("p a b c d -> p (a b c d)").rearrange("p (t c) -> p t c", t=T)
        tbank = [ps[:, 4 + b, 0:KI // 2].bitcast(F16) for b in range(2)]

        ld_x = [sem(f"ld_x{i}") for i in range(R)]
        ld_adj = [sem(f"ld_adj{i}") for i in range(STAGES)]
        ld_w0, ld_w3, ld_w1, ld_w2a, ld_w2b, ld_a, ld_b, ld_b12 = (sem(n) for n in (
            "ld_w0", "ld_w3", "ld_w1", "ld_w2a", "ld_w2b", "ld_a", "ld_b", "ld_b12"))
        s_cast = sem("s_cast")
        s_id0, s_id, s_one, s_nh = sem("s_id0"), sem("s_id"), sem("s_one"), sem("s_nh")
        s_wh, s_wl = sem("s_wh"), sem("s_wl")
        s_prod, s_wa, s_wah, s_was = sem("s_prod"), sem("s_wa"), sem("s_wah"), sem("s_was")
        s_xb = sem("s_xb")
        s_hi, s_lo = sem("s_hi"), sem("s_lo")
        s_t, s_xt = sem("s_t"), sem("s_xt")
        s_w, s_ph, s_c = sem("s_w"), sem("s_ph"), sem("s_c")
        s_acc, s_sum = sem("s_acc"), sem("s_sum")
        s_deg, s_degp, s_dis, s_disw = sem("s_deg"), sem("s_degp"), sem("s_dis"), sem("s_disw")
        s_u, s_v, s_h = sem("s_u"), sem("s_v"), sem("s_h")
        s_stat, s_aggr, s_ve, s_rstd, s_norm = (sem(n) for n in ("s_stat", "s_aggr", "s_ve", "s_rstd", "s_norm"))
        s_dmx, s_dmb, s_bias, s_gb, s_bw, s_bh, s_bl = (sem(n) for n in (
            "s_dmx", "s_dmb", "s_bias", "s_gb", "s_bw", "s_bh", "s_bl"))
        s_ht, s_yh, s_yl = sem("s_ht"), sem("s_yh"), sem("s_yl")
        s_srow = sem("s_srow")
        ld_rho = [sem(f"ld_rho{i}") for i in range(2)]
        s_rx, s_rho = sem("s_rx"), sem("s_rho")
        s_e, s_a, s_ah = sem("s_e"), sem("s_a"), sem("s_ah")
        s_al = [sem("s_al_dve"), sem("s_al_pool")]
        s_mm = sem("s_mm")
        s_z = sem("s_z")
        s_rd, s_ev = sem("s_rd"), sem("s_ev")
        s_out = sem("s_out")

        def tiles(eng, lo, hi, body):
            t = lo
            while t % R and t < hi:
                body(t, t % R)
                t += 1
            if hi - t > R:
                with eng.Fori(t // R, hi // R) as r:
                    for u in range(R):
                        body(r * R + u, u)
            else:
                for u in range(t, hi):
                    body(u, u % R)

        def pairs(eng, body, after):
            body(0, 0)
            with eng.Fori(0, PAIRS // 2 - 1) as c:
                body(c * 2 + 1, 1)
                body(c * 2 + 2, 0)
            body(PAIRS - 1, 1)
            after(PAIRS - 1)

        at = bass.ds
        block = ctx.enter_context(nc.Block())

        @block.sync
        def _(sp):
            adj_n = adj_in.rearrange("c h p w -> (c h) p w")
            for s in range(STAGES):
                sp.dma_start(stage[:, s, :], adj_n[s]).then_inc(ld_adj[s], 16)
            with sp.Fori(1, NL // STAGES) as r:
                for s in range(STAGES):
                    sp.wait_ge(s_cast, r * STAGES + (s - STAGES + 1))
                    sp.dma_start(stage[:, s, :], adj_n[at(r * STAGES + s, 1)].rearrange("a p w -> p (a w)"))\
                      .then_inc(ld_adj[s], 16)
            sp.wait_ge(s_ph, 2 * T)
            sp.dma_start(s_dram, srow).then_inc(s_srow, 16)
            sp.wait_ge(s_srow, 16)

            def load_rho(chunk, b):
                for hh in range(2):
                    sp.dma_start(rho[:, b, hh, :], s_dram[2 * b + hh:2 * b + hh + 1, at(chunk * CH, CH)]
                                 .partition_broadcast(P)).then_inc(ld_rho[b], 16)

            load_rho(0, 0)
            load_rho(0, 1)
            with sp.Fori(1, N // CH) as c:
                for b in range(2):
                    sp.wait_ge(s_a, c * (2 * T) + (b - 1) * T)
                    load_rho(c, b)

            def store(t, u):
                sp.wait_ge(s_norm, t + (3 * T + 1))
                sp.dma_start(out.rearrange("(t p) d -> t p d", p=P)[at(t, 1)].rearrange("a p d -> p (a d)"),
                             x[:, at(t, 1), :].rearrange("p a d -> p (a d)")).then_inc(s_out, 16)
            tiles(sp, 0, T, store)
            sp.wait_ge(s_out, 16 * T)

        prep_w = {0: w0, 2: w2a, 3: w2b, 4: w3}

        def tile_of(buf, t):
            return buf[:, at(t, 1), :].rearrange("p a f -> p (a f)")

        @block.scalar
        def _(act):
            xr = x_in.rearrange("(t p) d -> p t d", p=P)
            act.dma_start(w0f, w0_in.rearrange("(k p) h e -> p k (h e)", p=P)).then_inc(ld_w0, 16)
            for r in range(R):
                act.dma_start(x[:, r * R:(r + 1) * R, :], xr[:, r * R:(r + 1) * R, :]).then_inc(ld_x[r], 16)
            act.dma_start(bias0, b0_in.rearrange("(a n) -> a n", a=1).partition_broadcast(P)).then_inc(ld_b, 16)
            act.dma_start(w1f, w1_in.rearrange("(k p) (h f) -> p k h f", p=P, h=H)).then_inc(ld_w1, 16)
            act.dma_start(abc.rearrange("p h s f -> p (h s f)"),
                          a_in.rearrange("h f a -> (f a) h").rearrange("f h -> h f").rearrange("(b h) f -> b (h f)", b=1)
                          .partition_broadcast(P)).then_inc(ld_a, 16)
            act.dma_start(part(r_flat, (0, 4 * D), F32, "p (c f) -> p c f", c=4),
                          w2a_in.rearrange("(c p) f -> p c f", p=P)).then_inc(ld_w2a, 16)
            act.dma_start(part(r_flat, (4 * D, 8 * D), F32, "p (c f) -> p c f", c=4),
                          w2b_in.rearrange("(c p) f -> p c f", p=P)).then_inc(ld_w2b, 16)
            act.dma_start(w3f, w3_in.rearrange("(k p) f -> p k f", p=P)).then_inc(ld_w3, 16)

            act.wait_ge(ld_w0, 16)
            nc.scalar.activation(w0[:, 0, :, :], w0f, ACT.Copy, scale=WS).then_inc(s_wh, 1)

            def split_hi(k, t, u, src, ready):
                ready(act)
                if not (k == 0 and isinstance(t, int) and t < R):
                    act.wait_ge(s_t, t + (k * T - R + 1))
                nc.scalar.activation(xs[:, u, 0, :], tile_of(src, t), ACT.Copy).then_inc(s_hi, 1)

            def take_t(k, t, u):
                act.wait_ge(s_t, t + (k * T + 1))
                nc.scalar.activation(tile_of(xt, t), tbank[u % 2], ACT.Copy).then_inc(s_xt, 1)

            def take_p(k, t, u):
                act.wait_ge(s_w, t + (k * T + 1))
                b = ps[:, 6 + u % 2, :]
                if k == 1:
                    nc.scalar.activation(srow[:, at(t * P, P)], b[0:H, P:2 * P], ACT.Copy, scale=1 / WS)\
                      .then_inc(s_ph, 1)
                    return
                dst = pset[k % 2][:, at(t, 1), 0, 0:D].rearrange("p a f -> p (a f)")
                src = b[:, D:2 * D] if k in (2, 3) else b[:, 0:D]
                nc.scalar.activation(dst, src, ACT.Copy, scale=disw[:, at(t, 1)] if k == 4 else 1 / WS)\
                  .then_inc(s_ph, 1)

            def joint(k, src, ready):
                def one(t, u):
                    split_hi(k, t, u, src, lambda e: ready(e, t))
                    take_t(k, t - 1, (u - 1) % R)
                    take_p(k, t - 1, (u - 1) % R)
                split_hi(k, 0, 0, src, lambda e: ready(e, 0))
                tiles(act, 1, T, one)
                take_t(k, T - 1, R - 1)
                take_p(k, T - 1, R - 1)

            def lagged(k, src, ready):
                for t in range(R):
                    split_hi(k, t, t, src, lambda e: ready(e, t))

                def one(t, u):
                    take_t(k, t - R, u)
                    take_p(k, t - R, u)
                    split_hi(k, t, u, src, lambda e: ready(e, t))
                tiles(act, R, T, one)
                for t in range(T - R, T):
                    take_t(k, t, t % R)
                    take_p(k, t, t % R)

            for t in range(T + 1):
                if t < T:
                    split_hi(0, t, t % R, x, lambda e: e.wait_ge(ld_x[t // R], 16))
                if t > 0:
                    take_t(0, t - 1, (t - 1) % R)
                    take_p(0, t - 1, (t - 1) % R)
            act.wait_ge(s_w, T)
            for n, bi in enumerate((b1_in, b2_in)):
                act.dma_start(b12[:, n, :], bi.rearrange("(a n) -> a n", a=1).partition_broadcast(P)).then_inc(ld_b12, 16)
            act.wait_ge(ld_w1, 16)
            nc.scalar.activation(w1[:, 0, :, :], w1f.rearrange("p k h f -> p k (h f)"), ACT.Copy, scale=WS).then_inc(s_wh, 1)
            for buf, src, s in ((w2a, w2af, ld_w2a), (w2b, w2bf, ld_w2b)):
                act.wait_ge(s, 16)
                nc.scalar.activation(buf[:, 0, :, :].rearrange("p k (s f) -> p k s f", s=2), src, ACT.Copy, scale=WS)\
                  .then_inc(s_wh, 1)
            act.wait_ge(ld_w3, 16)
            nc.scalar.activation(w3[:, 0, :, :], w3f, ACT.Copy, scale=WS).then_inc(s_wh, 1)
            act.wait_ge(s_wa, 2 * K2)
            nc.scalar.activation(was[:, 0], wa[:, :, :, :], ACT.Copy, scale=WS).then_inc(s_wah, 1)

            act.wait_ge(s_wl, 5)
            lagged(1, x, lambda e, t: e.wait_ge(s_norm, t + 1))

            act.wait_ge(s_bias, 2)
            for h in range(H):
                nc.scalar.activation(bet[:, h, :], dall[:, :, h], ACT.Exp, scale=SLOPE, bias=bias_b[:, h:h + 1])\
                  .then_inc(s_gb, 1)
            for h in range(H):
                nc.scalar.activation(gam[:, h, :], dall[:, :, h], ACT.Exp, scale=1 - SLOPE, bias=bias_g[:, h:h + 1])\
                  .then_inc(s_gb, 1)

            def rho_exp(p, b):
                chunk16 = p // 2 if isinstance(p, int) else None
                act.wait_ge(ld_rho[b], 32 * (chunk16 + 1) if chunk16 is not None else (p + (2 - b)) * 16)
                if isinstance(p, int) and p < 2:
                    pass
                for hh in range(2):
                    h = 2 * b + hh
                    ins = nc.scalar.activation(rho[:, b, hh, :], rho[:, b, hh, :], ACT.Exp, scale=-(1 - SLOPE),
                                               bias=bias_g[:, h:h + 1])
                ins.then_inc(s_rx, 1)

            act.wait_ge(s_bw, 1)

            def value_hi(t, u):
                for half in range(2):
                    act.wait_ge(s_ht, t * 2 + (half + 1))
                    for hh in range(2):
                        h = 2 * half + hh
                        ins = nc.scalar.activation(
                            val[0][:, at(t, 1), h, 0:D].rearrange("p a f -> p (a f)"),
                            ps[:, 2 * u + half, hh * D:(hh + 1) * D], ACT.Copy, scale=betw[:, h, at(t, 1)])
                    ins.then_inc(s_yh, 1)
            tiles(act, 0, T, value_hi)
            rho_exp(0, 0)

            def exp_adj(p, q, jt):
                chunk = (p - q) // 2 if isinstance(p, int) else None
                n = p * T + jt
                if not isinstance(n, int) or n >= 2:
                    act.wait_ge(s_a, n - 1)
                col = chunk * CH if chunk is not None else (p - q) * (CH // 2)
                nc.scalar.activation(ring_e[:, jt % 2, :], adj[:, jt, at(col, CH)], ACT.Exp).then_inc(s_e, 1)

            def att_hi(p, jt):
                act.wait_ge(s_a, p * T + (jt + 1))
                if jt > 3:
                    act.wait_ge(s_mm, p * (T - 1) + (jt - 3))
                elif isinstance(p, int) and p == 0:
                    act.wait_ge(s_ht, 2 * T)
                elif jt == 3:
                    act.wait_ge(s_z, p * (2 * R))
                else:
                    act.wait_ge(s_mm, p * (T - 1) + (jt - 2))
                nc.scalar.activation(ring_hl[:, jt % 4, 0], ring_a[:, jt % 2], ACT.Copy).then_inc(s_ah, 1)

            def pair(p, q):
                for jt in range(T):
                    exp_adj(p, q, jt)
                    if jt > 0:
                        att_hi(p, jt - 1)
                    elif not isinstance(p, int) or p > 0:
                        att_hi(p - 1, T - 1)
                    if jt == 8 and not (isinstance(p, int) and p == PAIRS - 1):
                        rho_exp(p + 1, 1 - q)
            pairs(act, pair, lambda p: att_hi(p, T - 1))

            act.wait_ge(s_al[0], STEPS // 2)
            act.wait_ge(s_al[1], STEPS // 2)
            joint(2, x, lambda e, t: e.wait_ge(s_norm, t + (T + 1)))
            lagged(3, hid, lambda e, t: e.wait_ge(s_h, t + 1))
            lagged(4, x, lambda e, t: e.wait_ge(s_norm, t + (2 * T + 1)))

        @block.tensor
        def _(pe):
            def transpose(k, t, u):
                pe.wait_ge(s_lo, t + (k * T + 1))
                if not (isinstance(t, int) and k == 0 and t < 2):
                    pe.wait_ge(s_xt, t + (k * T - 1))
                for c in range(2 * K2):
                    ins = nc.tensor.transpose(tbank[u % 2][:, c * P:(c + 1) * P],
                                              xs[:, u, c // K2, (c % K2) * P:(c % K2 + 1) * P], ident[:, :])
                ins.then_inc(s_t, 1)

            TERMS = [(0, 0), (0, 1), (1, 0)]

            def project(k, t, u):
                pe.wait_ge(s_xt, t + (k * T + 1))
                if not (isinstance(t, int) and k == 0 and t < 2):
                    pe.wait_ge(s_c, t + (k * T - 1))
                xtt = tile_of(xt, t)
                bank = ps[:, 6 + u % 2, :]

                def xpart(a, kk):
                    return xtt[:, (a * K2 + kk) * P:(a * K2 + kk + 1) * P]
                steps = [(a, b, kk) for kk in range(K2) for a, b in TERMS]
                if k == 1:
                    for n, (a, b, kk) in enumerate(steps):
                        nc.tensor.matmul(bank[:, 0:H], xpart(a, kk), was[:, b, kk, 1, :],
                                         start=(n == 0), stop=(n == len(steps) - 1))
                    for n, (a, b, kk) in enumerate(steps):
                        ins = nc.tensor.matmul(bank[0:H, P:2 * P], was[:, b, kk, 0, :], xpart(a, kk),
                                               start=(n == 0), stop=(n == len(steps) - 1))
                    ins.then_inc(s_w, 1)
                    return
                w = prep_w[k]
                width = w.shape[3]
                for n, (a, b, kk) in enumerate(steps):
                    ins = nc.tensor.matmul(bank[:, 0:width], xpart(a, kk), w[:, b, kk, :],
                                           start=(n == 0), stop=(n == len(steps) - 1))
                ins.then_inc(s_w, 1)

            def agg_step(a, k, it, bank, j, done):
                width = D + 1 if a == 0 else D
                pp = pset[k % 2]
                lhs = adj[:, j, at(it * P, P)]
                nc.tensor.matmul(ps[:, bank, 0:width], lhs, pp[:, j, 0, 0:width], start=(j == 0), stop=False)
                ins = nc.tensor.matmul(ps[:, bank, 0:D], lhs, pp[:, j, 1, 0:D], start=False, stop=(j == T - 1))
                if done:
                    ins.then_inc(s_acc, 1)

            def group0(a, k, js):
                for j in js:
                    pe.wait_ge(s_c, k * T + j + 1)
                    for it in range(R):
                        if j == 0 and a > 0:
                            pe.wait_ge(s_sum, (a - 1) * T + T - R + it + 1)
                        agg_step(a, k, it, it, j, j == T - 1)

            def joint(k, a, before_agg):
                transpose(k, 0, 0)
                for t in range(T):
                    if t + 1 < T:
                        transpose(k, t + 1, (t + 1) % R)
                    project(k, t, t % R)
                    if t == T // 2:
                        before_agg()
                    if t >= T // 2:
                        j0 = 2 * (t - T // 2)
                        group0(a, k, [j for j in (j0 - 1, j0) if j >= 0])
                group0(a, k, [T - 1])

            def rest(a, knext, ready):
                k = (0, 2, 3, 4)[a]

                def one(t, u):
                    ready(t, u)
                    pe.wait_ge(s_sum, t + (a * T - R + 1))
                    for j in range(T):
                        if j == T - 4 and knext is not None:
                            transpose(knext, t - R, u)
                        agg_step(a, k, t, u, j, j == T - 1)
                    if knext is not None:
                        project(knext, t - R, u)
                tiles(pe, R, T, one)

            def tail(k, a):
                e = T - R
                plan = [([0, 1, 2, 3], e, None), ([4, 5], e + 1, e), ([6, 7], e + 2, e + 1),
                        ([8, 9], e + 3, e + 2), ([10, 11], None, e + 3), (list(range(e, T)), None, None)]
                for js, tt, tp in plan:
                    if a is not None:
                        group0(a, k, js)
                    if tt is not None:
                        transpose(k, tt, tt % R)
                    if tp is not None:
                        project(k, tp, tp % R)

            pe.wait_ge(s_id, 1)
            pe.wait_ge(s_wl, 1)
            joint(0, 0, lambda: (pe.wait_ge(s_cast, 4), pe.wait_ge(s_one, 1)))

            def cast_ready(t, u):
                pe.wait_ge(s_cast, t + 2 if u % 2 == 0 else t + 1)
            pe.wait_ge(s_was, 1)
            rest(0, 1, cast_ready)
            tail(1, None)

            pe.wait_ge(s_sum, T)
            pe.wait_ge(s_c, 2 * T)

            def values(t, u):
                xtt = tile_of(xt, t)
                for half in range(2):
                    if not (isinstance(t, int) and t < R):
                        pe.wait_ge(s_yl, t * 2 + (half + 1 - 2 * R))
                    steps = [(a, b, kk) for kk in range(K2) for a, b in TERMS]
                    for n, (a, b, kk) in enumerate(steps):
                        ins = nc.tensor.matmul(ps[:, 2 * u + half, :],
                                               xtt[:, (a * K2 + kk) * P:(a * K2 + kk + 1) * P],
                                               w1[:, b, kk, half * 512:(half + 1) * 512],
                                               start=(n == 0), stop=(n == len(steps) - 1))
                    ins.then_inc(s_ht, 1)
            for t in range(R):
                values(t, t)
            tiles(pe, R, T, values)

            pe.wait_ge(s_bl, 1)
            pe.wait_ge(s_yl, 2 * T)

            def pair(p, q):
                first = isinstance(p, int) and p == 0
                for jt in range(T):
                    pe.wait_ge(s_al[jt % 2], p * (T // 2) + (jt // 2 + 1))
                    for b in range(2 * R):
                        hh, it = b // R, b % R
                        if jt == 0 and not first:
                            pe.wait_ge(s_ev, p * (2 * R) + (b + 1 - 2 * R))
                        h = 2 * q + hh
                        hi = ring_hl[:, jt % 4, 0, hh, it * P:(it + 1) * P]
                        lo = ring_hl[:, jt % 4, 1, hh, it * P:(it + 1) * P]
                        acc = ps[:, b, 0:D + 1]
                        nc.tensor.matmul(acc, hi, val[0][:, jt, h, 0:D + 1], start=(jt == 0), stop=False)
                        nc.tensor.matmul(acc, hi, val[1][:, jt, h, 0:D + 1], start=False, stop=False)
                        ins = nc.tensor.matmul(acc, lo, val[0][:, jt, h, 0:D + 1], start=False, stop=(jt == T - 1))
                        if jt == T - 1:
                            ins.then_inc(s_z, 1)
                    if jt < T - 1:
                        ins.then_inc(s_mm, 1)
            pairs(pe, pair, lambda p: None)

            joint(2, 1, lambda: pe.wait_ge(s_ev, 2 * R * PAIRS))
            rest(1, 3, lambda t, u: None)
            tail(3, 2)
            rest(2, 4, lambda t, u: None)
            tail(4, 3)
            rest(3, None, lambda t, u: None)

        @block.vector
        def _(dve):
            dve.wait_ge(s_wh, 1)
            nc.vector.scalar_tensor_tensor(w0[:, 1, :, :], w0f, WS, w0[:, 0, :, :], op0=ALU.mult, op1=ALU.subtract)\
              .then_inc(s_wl, 1)

            def cast(n, s, r):
                dve.wait_ge(ld_adj[s], r * 16)
                src = stage[:, s, :].rearrange("p (j w) -> p j w", j=JH)
                nc.vector.tensor_copy(adj[:, (s % 2) * JH:(s % 2 + 1) * JH, at(n, LW)], src).then_inc(s_cast, 1)

            def cast_n(n):
                cast((n // 2) * LW, n % STAGES, n // STAGES + 1)

            def split_lo(k, t, u, src):
                dve.wait_ge(s_hi, t + (k * T + 1))
                nc.vector.tensor_sub(xs[:, u, 1, :], tile_of(src, t), xs[:, u, 0, :]).then_inc(s_lo, 1)

            def take(k, t, u):
                dve.wait_ge(s_ph, t + (k * T + 1))
                b = ps[:, 6 + u % 2, :]
                if k == 1:
                    nc.vector.tensor_scalar(tile_of(dall, t), b[:, 0:H], 1 / WS, None, ALU.mult).then_inc(s_c, 1)
                    return
                hi = pset[k % 2][:, at(t, 1), 0, 0:D].rearrange("p a f -> p (a f)")
                lo = pset[k % 2][:, at(t, 1), 1, 0:D].rearrange("p a f -> p (a f)")
                ot = tile_of(own, t)
                if k in (2, 3):
                    nc.vector.scalar_tensor_tensor(ot, b[:, 0:D], 1 / WS, b12[:, k - 2, :],
                                                   op0=ALU.mult, op1=ALU.add)
                if k == 4:
                    nc.vector.tensor_scalar(ot, b[:, 0:D], disw[:, at(t, 1)], None, ALU.mult)
                src = b[:, D:2 * D] if k in (2, 3) else b[:, 0:D]
                nc.vector.scalar_tensor_tensor(lo, src, disw[:, at(t, 1)] if k == 4 else 1 / WS, hi,
                                               op0=ALU.mult, op1=ALU.subtract).then_inc(s_c, 1)

            def hold(s, value):
                dve.wait_ge(s, value)
                nc.vector.memset(held[:, :], 0.0)

            def statistics(l, slot):
                nc.vector.bn_stats(stat[:, slot, :], total[:, slot, :]).then_inc(s_stat, 1)
                hold(s_stat, l + 1)
                nc.vector.bn_aggr(mv[:, slot, :], stat[:, slot, :]).then_inc(s_aggr, 1)

            def normalise(l, slot, xt_):
                dve.wait_ge(s_rstd, l + 1)
                nc.vector.tensor_scalar(xt_, total[:, slot, :], mv[:, slot, 0:1], rstd[:, slot:slot + 1],
                                        ALU.subtract, ALU.mult).then_inc(s_norm, 1)

            def take_sum(a, t, u):
                q = t + a * T
                dve.wait_ge(s_acc, q + 1)
                acc = ps[:, u, 0:D]
                xt_ = tile_of(x, t)
                if a == 0:
                    dve.wait_ge(s_xb, T)
                    nc.vector.tensor_copy(deg[:, at(t, 1)], ps[:, u, D:D + 1]).then_inc(s_deg, 1)
                    nc.vector.tensor_tensor(total[:, u, :], acc, xt_, ALU.add).then_inc(s_sum, 1)
                    dve.wait_ge(s_sum, q + 1)
                    statistics(t, u)
                    return
                ot, ht_ = tile_of(own, t), tile_of(hid, t)
                if a == 1:
                    nc.vector.tensor_tensor(ht_, acc, ot, ALU.add).then_inc(s_sum, 1)
                    dve.wait_ge(s_sum, q + 1)
                    nc.vector.tensor_scalar(ht_, ht_, 0.0, None, ALU.max).then_inc(s_h, 1)
                    return
                nc.vector.tensor_tensor(ot, acc, ot, ALU.add).then_inc(s_sum, 1)
                dve.wait_ge(s_sum, q + 1)
                l = t + (a - 2) * T
                if a == 2:
                    nc.vector.scalar_tensor_tensor(ot, ot, 0.0, ht_, op0=ALU.max, op1=ALU.add).then_inc(s_u, 1)
                    dve.wait_ge(s_u, l + 1)
                    nc.vector.scalar_tensor_tensor(total[:, u, :], ot, 0.0, xt_, op0=ALU.max, op1=ALU.add).then_inc(s_v, 1)
                else:
                    nc.vector.tensor_scalar(ot, ot, dis[:, at(t, 1)], 0.0, ALU.mult, ALU.max).then_inc(s_u, 1)
                    dve.wait_ge(s_u, l + 1)
                    nc.vector.tensor_tensor(total[:, u, :], ot, xt_, ALU.add).then_inc(s_v, 1)
                dve.wait_ge(s_v, l + 1)
                statistics(t + a * T, u)

            def finish(a, k, t, u):
                if a != 1:
                    normalise(t + a * T, u, tile_of(x, t))
                if k is not None:
                    split_lo(k, t, u, hid if a == 1 else x)

            def aggregate(a, k, extra=lambda r, u: None):
                for t in range(R):
                    take_sum(a, t, t)
                    finish(a, k, t, t)

                def one(t, u):
                    extra(t, u)
                    take_sum(a, t, u)
                    if k is not None:
                        take(k, t - R, u)
                    finish(a, k, t, u)
                tiles(dve, R, T, one)
                if k is not None:
                    for t in range(T - R, T):
                        take(k, t, t % R)

            CASTS_AT = {4: 0, 5: 1, 7: 2, 8: 3, 10: 4, 12: 5, 14: 6}
            for t in range(T):
                if t % R == 0:
                    dve.wait_ge(ld_x[t // R], 16)
                split_lo(0, t, t % R, x)
                if t > 0:
                    take(0, t - 1, (t - 1) % R)
                if t in CASTS_AT:
                    cast_n(CASTS_AT[t])
            take(0, T - 1, (T - 1) % R)
            cast_n(7)
            for n, (buf, src) in enumerate(((w1, w1f.rearrange("p k h f -> p k (h f)")), (w2a, w2af), (w2b, w2bf), (w3, w3f))):
                dve.wait_ge(s_wh, n + 2)
                for kk in range(K2):
                    hi, lo = buf[:, 0, kk, :], buf[:, 1, kk, :]
                    if n in (1, 2):
                        hi, lo = (v.rearrange("p (s f) -> p s f", s=2) for v in (hi, lo))
                    ins = nc.vector.scalar_tensor_tensor(lo, src[:, kk], WS, hi, op0=ALU.mult, op1=ALU.subtract)
                ins.then_inc(s_wl, 1)
            cast_n(8)
            dve.wait_ge(ld_a, 16)
            n = 0
            for kk in range(K2):
                for s in range(2):
                    if n:
                        dve.wait_ge(s_wa, n)
                    nc.vector.tensor_tensor(prod, w1f[:, kk], abc[:, :, s, :], ALU.mult).then_inc(s_prod, 1)
                    n += 1
                    dve.wait_ge(s_prod, n)
                    nc.vector.reduce_sum(wa[:, kk, s, :], prod, axis=AX.X).then_inc(s_wa, 1)
            cast_n(9)
            dve.wait_ge(s_wah, 1)
            nc.vector.scalar_tensor_tensor(was[:, 1], wa[:, :, :, :], WS, was[:, 0], op0=ALU.mult, op1=ALU.subtract)\
              .then_inc(s_was, 1)

            for t in range(R):
                take_sum(0, t, t)
                finish(0, 1, t, t)
            for r in range(1, T // R):
                for half in range(2):
                    cast_n(8 + 2 * r + half)
                for u in range(R):
                    t = r * R + u
                    take_sum(0, t, u)
                    take(1, t - R, u)
                    finish(0, 1, t, u)
            for t in range(T - R, T):
                take(1, t, t % R)

            dve.wait_ge(s_c, 2 * T)
            nc.vector.reduce_max(dmx[:, :], dall[:, :, :].rearrange("p t h -> p h t"), axis=AX.X).then_inc(s_dmx, 1)
            dve.wait_ge(s_dmb, 1)
            nc.vector.tensor_scalar(bias_b[:, :], dmb[:, :], -SLOPE, None, ALU.mult).then_inc(s_bias, 1)
            nc.vector.tensor_scalar(bias_g[:, :], dmb[:, :], -(1 - SLOPE), LCAP, ALU.mult, ALU.add).then_inc(s_bias, 1)
            dve.wait_ge(s_gb, H)
            nc.vector.tensor_scalar(betw[:, :, :], bet[:, :, :], 1 / WS, None, ALU.mult).then_inc(s_bw, 1)
            nc.vector.tensor_scalar(bet4[:, :, :], bet[:, :, :], float(H), None, ALU.mult).then_inc(s_bw, 1)
            dve.wait_ge(s_bw, 2)

            def value_lo(t, u):
                for half in range(2):
                    dve.wait_ge(s_yh, t * 2 + (half + 1))
                    for hh in range(2):
                        h = 2 * half + hh
                        ins = nc.vector.scalar_tensor_tensor(
                            val[1][:, at(t, 1), h, 0:D].rearrange("p a f -> p (a f)"),
                            ps[:, 2 * u + half, hh * D:(hh + 1) * D], betw[:, h, at(t, 1)],
                            val[0][:, at(t, 1), h, 0:D].rearrange("p a f -> p (a f)"),
                            op0=ALU.mult, op1=ALU.subtract)
                    ins.then_inc(s_yl, 1)
            value_lo(0, 0)
            b4 = bet4[:, :, :].rearrange("p h t -> p t h")
            nc.vector.tensor_copy(val[0][:, :, :, D], b4).then_inc(s_bh, 1)
            dve.wait_ge(s_bh, 1)
            nc.vector.tensor_tensor(val[1][:, :, :, D], b4, val[0][:, :, :, D], ALU.subtract).then_inc(s_bl, 1)
            for t in range(1, R):
                value_lo(t, t)
            tiles(dve, R, T, value_lo)
            dve.wait_ge(s_gb, 2 * H)

            def cap_rho(p, b):
                dve.wait_ge(s_rx, p + 1)
                nc.vector.tensor_scalar(rho[:, b], rho[:, b], math.exp(LCAP), None, ALU.min).then_inc(s_rho, 1)
            cap_rho(0, 0)

            def weights(p, q, jt):
                n = p * T + jt
                if jt == 0:
                    dve.wait_ge(s_rho, p + 1)
                dve.wait_ge(s_e, n + 1)
                if not isinstance(n, int) or n >= 2:
                    dve.wait_ge(s_ah, n - 1)
                    dve.wait_ge(s_al[jt % 2], p * (T // 2) + jt // 2)
                for hh in range(2):
                    h = 2 * q + hh
                    ins = nc.vector.scalar_tensor_tensor(
                        ring_a[:, jt % 2, hh, :], rho[:, q, hh, :], gam[:, h, jt:jt + 1], ring_e[:, jt % 2, :],
                        op0=ALU.max, op1=ALU.mult)
                ins.then_inc(s_a, 1)

            def att_lo(m, jt):
                dve.wait_ge(s_ah, m + 1)
                nc.vector.tensor_sub(ring_hl[:, jt % 4, 1], ring_a[:, jt % 2], ring_hl[:, jt % 4, 0])\
                  .then_inc(s_al[0], 1)

            def take_attention(p, q):
                first = (p - q) * 2
                for g in range(2):
                    dve.wait_ge(s_z, p * (2 * R) + (g + 1) * R)
                    nc.vector.reciprocal(rden[:, g * R:(g + 1) * R], ps[:, g * R:(g + 1) * R, D]).then_inc(s_rd, 1)
                    dve.wait_ge(s_rd, p * 2 + (g + 1))
                    for it in range(R):
                        b = g * R + it
                        if g == 1:
                            dve.wait_ge(s_ev, p * (2 * R) + (it + 1))
                        xt_ = tile_of(x, first + it)
                        dst = total[:, it, :] if q == 1 and g == 1 else xt_
                        nc.vector.scalar_tensor_tensor(dst, ps[:, b, 0:D], rden[:, b:b + 1], xt_,
                                                       op0=ALU.mult, op1=ALU.add).then_inc(s_ev, 1)

            def chunk_statistics(p):
                first = (p - 1) * 2
                dve.wait_ge(s_ev, p * (2 * R) + 2 * R)
                for it in range(R):
                    statistics(first + (T + it), it)

            def chunk_normalise(p):
                first = (p - 1) * 2
                for it in range(R):
                    normalise(first + (T + it), it, tile_of(x, first + it))

            def pair(p, q):
                first = isinstance(p, int) and p == 0
                for jt in range(T):
                    weights(p, q, jt)
                    if jt % 2 == 1:
                        att_lo(p * T + (jt - 1), jt - 1)
                    if not first:
                        if jt == 3:
                            take_attention(p - 1, 1 - q)
                        if q == 0 and jt == 5:
                            chunk_statistics(p - 1)
                        if q == 0 and jt == 8:
                            chunk_normalise(p - 1)
                    if jt == 12 and not (isinstance(p, int) and p == PAIRS - 1):
                        cap_rho(p + 1, 1 - q)

            def end(p):
                take_attention(p, 1)
                chunk_statistics(p)
                chunk_normalise(p)
            pairs(dve, pair, end)

            dve.wait_ge(ld_b12, 32)
            for t in range(R):
                split_lo(2, t, t, x)
                if t > 0:
                    take(2, t - 1, t - 1)

            def one(t, u):
                split_lo(2, t, u, x)
                take(2, t - 1, (u - 1) % R)
            tiles(dve, R, T, one)
            take(2, T - 1, R - 1)
            aggregate(1, 3)
            aggregate(2, 4)
            aggregate(3, None)

        @block.gpsimd
        def _(pool):
            nc.gpsimd.memset(ident[:, :], 0.0).then_inc(s_id0, 1)
            nc.gpsimd.memset(pset[0][:, :, 0, D:D + 1], 1.0).then_inc(s_one, 1)
            pool.wait_ge(s_id0, 1)
            nc.gpsimd.affine_select(out=ident[:, :], in_=ident[:, :], compare_op=ALU.not_equal, fill=1.0, base=0,
                                    pattern=[[-1, P]], channel_multiplier=1).then_inc(s_id, 1)
            nc.gpsimd.memset(neghalf[:, :], -0.5).then_inc(s_nh, 1)
            nc.gpsimd.memset(epsv[:, :], EPS).then_inc(s_nh, 1)
            pool.wait_ge(s_nh, 2)
            pool.wait_ge(ld_b, 16)

            def add_b0(t, u):
                pool.wait_ge(s_lo, t + 1)
                nc.gpsimd.tensor_tensor(tile_of(x, t), tile_of(x, t), bias0, ALU.add).then_inc(s_xb, 1)
            tiles(pool, 0, T, add_b0)

            def inv_std(l, slot):
                pool.wait_ge(s_aggr, l + 1)
                nc.gpsimd.tensor_tensor(veps[:, slot:slot + 1], mv[:, slot, 1:2], epsv[:, :], ALU.add).then_inc(s_ve, 1)
                pool.wait_ge(s_ve, l + 1)
                nc.gpsimd.tensor_tensor(rstd[:, slot:slot + 1], veps[:, slot:slot + 1], neghalf[:, 0:1], ALU.pow)\
                  .then_inc(s_rstd, 1)
            tiles(pool, 0, T, inv_std)
            pool.wait_ge(s_dmx, 1)
            nc.gpsimd.partition_all_reduce(dmb[:, :], dmx[:, :], P, bass.bass_isa.ReduceOp.max).then_inc(s_dmb, 1)
            pool.wait_ge(s_deg, T)
            nc.gpsimd.tensor_scalar(degp[:, :], deg[:, :], 1.0, None, ALU.add).then_inc(s_degp, 1)
            pool.wait_ge(s_degp, 1)
            nc.gpsimd.tensor_tensor(dis[:, :], degp[:, :], neghalf[:, :], ALU.pow).then_inc(s_dis, 1)
            pool.wait_ge(s_dis, 1)
            nc.gpsimd.tensor_scalar(disw[:, :], dis[:, :], 1 / WS, None, ALU.mult).then_inc(s_disw, 1)

            def att_lo(m, jt):
                pool.wait_ge(s_ah, m + 1)
                nc.gpsimd.tensor_sub(ring_hl[:, jt % 4, 1], ring_a[:, jt % 2], ring_hl[:, jt % 4, 0])\
                  .then_inc(s_al[1], 1)

            def pair(p, q):
                first = isinstance(p, int) and p == 0
                for jt in range(1, T, 2):
                    att_lo(p * T + jt, jt)
                    if jt == 5 and q == 0 and not first:
                        for it in range(R):
                            inv_std((p - 2) * 2 + (T + it), it)
            pairs(pool, pair, lambda p: [inv_std((p - 1) * 2 + (T + it), it) for it in range(R)])
            tiles(pool, 2 * T, 4 * T, inv_std)


_ORDER = ["x", "adj", "L0_gnn_W", "L0_gnn_b", "L1_gnn_W", "L1_gnn_a", "L2_gnn_W1", "L2_gnn_b1", "L2_gnn_W2",
          "L2_gnn_b2", "L3_gnn_W"]


def kernel(**inputs):
    import numpy as np
    import concourse.bacc as bacc
    from concourse import mybir as _mybir
    from concourse.bass_utils import run_bass_kernel_spmd

    host = {k: np.asarray(inputs[k]) for k in _ORDER}
    n = host["adj"].shape[0]
    blocks, halves, p = 8, 2, 128
    host["adj"] = np.ascontiguousarray(
        host["adj"].T.reshape(halves, n // (halves * p), p, blocks, n // blocks).transpose(3, 0, 2, 1, 4)
        .reshape(blocks, halves, p, -1))
    host["L0_gnn_W"] = np.ascontiguousarray(host["L0_gnn_W"].transpose(1, 0, 2))
    host["L0_gnn_b"] = host["L0_gnn_b"].reshape(-1)

    nc = bacc.Bacc("TRN2", target_bir_lowering=False, num_devices=1)
    arrays, args = {}, []
    for k in _ORDER:
        a = np.ascontiguousarray(host[k])
        arrays[f"in_{k}"] = a
        args.append(nc.dram_tensor(f"in_{k}", a.shape, _mybir.dt.from_np(a.dtype), kind="ExternalInput").ap())
    args.append(nc.dram_tensor("out_x", host["x"].shape, _mybir.dt.float32, kind="ExternalOutput").ap())
    graph_stack(nc, *args)
    r = run_bass_kernel_spmd(nc, [arrays], core_ids=[0])
    return r.results[0]["out_x"]
```

```python
import math
from contextlib import ExitStack

import concourse.bass as bass
from concourse import mybir


def graph_stack(nc, x_in, adj_in, w0_in, b0_in, w1_in, a_in, w2a_in, b1_in, w2b_in, b2_in, w3_in, out):
    F32, F16, BF16 = mybir.dt.float32, mybir.dt.float16, mybir.dt.bfloat16
    ALU, ACT, AX = mybir.AluOpType, mybir.ActivationFunctionType, mybir.AxisListType

    P = 128
    N, D = x_in.shape
    T = N // P
    H, A2 = a_in.shape[0], a_in.shape[1]
    K2 = D // P
    KI = 2 * K2 * P
    R = 4
    CH = R * P
    PAIRS = (N // CH) * (H // 2)
    STEPS = PAIRS * T
    PW = D + 2
    WS = 64.0
    LCAP = 6 * math.log(2.0)
    SLOPE = 0.01
    EPS = 1e-5
    AHEAD = 3
    NL = 16
    LW = N // (NL // 2)
    JH = T // 2

    ctx = ExitStack()
    with ctx:
        def sb(name, shape, dt):
            return ctx.enter_context(nc.sbuf_tensor(name, shape, dt))

        def sem(name):
            return ctx.enter_context(nc.semaphore(name))

        adj = sb("adj", [P, T, N], BF16)
        x = sb("x", [P, T, D], F32)
        arena = sb("arena", [P, 2 * T * H * PW // 2], F32)
        w0 = sb("w0", [P, 2, K2, D], F16)
        w1 = sb("w1", [P, 2, K2, H * D], F16)
        w2a = sb("w2a", [P, 2, K2, 2 * D], F16)
        w2b = sb("w2b", [P, 2, K2, 2 * D], F16)
        w3 = sb("w3", [P, 2, K2, D], F16)
        rho = sb("rho", [P, 2, 2, CH], F32)
        ring_e = sb("ring_e", [P, 2, CH], F32)
        ring_a = sb("ring_a", [P, 2, 2, CH], F32)
        ring_hl = sb("ring_hl", [P, 4, 2, 2, CH], F16)
        ident = sb("ident", [P, P], F16)
        stat = sb("stat", [P, R, 6], F32)
        mv = sb("mv", [P, R, 2], F32)
        veps = sb("veps", [P, R], F32)
        rstd = sb("rstd", [P, R], F32)
        epsv = sb("epsv", [P, 1], F32)
        held = sb("held", [P, 1], F32)
        total = sb("total", [P, R, D], F32)
        b12 = w0[:, :, :, :].rearrange("p a k f -> p (a k f)").bitcast(F32).rearrange("p (a f) -> p a f", a=2)
        bias0 = total[:, R - 1, :]
        neghalf = sb("neghalf", [P, T], F32)
        deg = sb("deg", [P, T], F32)
        degp = sb("degp", [P, T], F32)
        dis = sb("dis", [P, T], F32)
        disw = sb("disw", [P, T], F32)
        wa = sb("wa", [P, K2, 2, H], F32)
        was = sb("was", [P, 2, K2, 2, H], F16)
        dall = sb("dall", [P, T, H], F32)
        dmx = sb("dmx", [P, H], F32)
        dmb = sb("dmb", [P, H], F32)
        bias_g = sb("bias_g", [P, H], F32)
        bias_b = sb("bias_b", [P, H], F32)
        gam = sb("gam", [P, H, T], F32)
        bet = sb("bet", [P, H, T], F32)
        betw = sb("betw", [P, H, T], F32)
        bet4 = sb("bet4", [P, H, T], F32)
        rden = sb("rden", [P, 2 * R], F32)
        ps = ctx.enter_context(nc.psum_tensor("ps", [P, 8, 512], F32))
        s_dram = nc.dram_tensor("s_scratch", [H, N], F32, kind="Internal").ap()

        def part(base, words, dt, text, **kw):
            v = base[:, words[0]:words[1]]
            if dt is not F32:
                v = v.bitcast(dt)
            return v.rearrange(text, **kw) if text else v

        PSET = T * 2 * PW // 2
        pset = [part(arena, (s * PSET, (s + 1) * PSET), F16, "p (t q f) -> p t q f", t=T, q=2) for s in range(2)]
        own = part(arena, (2 * PSET, 2 * PSET + T * D), F32, "p (t f) -> p t f", t=T)
        hid = part(arena, (2 * PSET + T * D, 2 * PSET + 2 * T * D), F32, "p (t f) -> p t f", t=T)
        STAGES = 4
        SW = JH * LW
        stage = part(arena, (PSET, PSET + STAGES * SW), F32, "p (s w) -> p s w", s=STAGES)
        w1f = part(arena, (PSET + STAGES * SW, PSET + STAGES * SW + K2 * H * D), F32, "p (k h f) -> p k h f", k=K2, h=H)
        o = PSET + STAGES * SW + K2 * H * D
        abc = part(arena, (o, o + H * A2), F32, "p (h s f) -> p h s f", h=H, s=2)
        VW = T * H * PW // 2
        val = [part(arena, (s * VW, (s + 1) * VW), F16, "p (t h f) -> p t h f", t=T, h=H) for s in range(2)]
        a_flat = ring_a[:, :, :, :].rearrange("p a b c -> p (a b c)")
        xs = part(a_flat, (0, R * D), F16, "p (s q f) -> p s q f", s=R, q=2)
        w0f = part(a_flat, (R * D, R * D + K2 * D), F32, "p (k f) -> p k f", k=K2)
        w3f = part(a_flat, (R * D + K2 * D, R * D + 2 * K2 * D), F32, "p (k f) -> p k f", k=K2)
        r_flat = rho[:, :, :, :].rearrange("p a b c -> p (a b c)")
        w2af = part(r_flat, (0, 4 * D), F32, "p (s k f) -> p k s f", s=2, k=K2)
        w2bf = part(r_flat, (4 * D, 8 * D), F32, "p (s k f) -> p k s f", s=2, k=K2)
        srow = r_flat[0:H, :]
        prod = ring_e[:, :, :].rearrange("p a (h f) -> p (a h) f", f=D)
        xt = ring_hl[:, :, :, :, :].rearrange("p a b c d -> p (a b c d)").rearrange("p (t c) -> p t c", t=T)
        tbank = [ps[:, 4 + b, 0:KI // 2].bitcast(F16) for b in range(2)]

        ld_x = [sem(f"ld_x{i}") for i in range(R)]
        ld_adj = [sem(f"ld_adj{i}") for i in range(STAGES)]
        ld_w0, ld_w3, ld_w1, ld_w2a, ld_w2b, ld_a, ld_b, ld_b12 = (sem(n) for n in (
            "ld_w0", "ld_w3", "ld_w1", "ld_w2a", "ld_w2b", "ld_a", "ld_b", "ld_b12"))
        s_cast = sem("s_cast")
        s_id0, s_id, s_one, s_nh = sem("s_id0"), sem("s_id"), sem("s_one"), sem("s_nh")
        s_wh, s_wl = sem("s_wh"), sem("s_wl")
        s_prod, s_wa, s_wah, s_was = sem("s_prod"), sem("s_wa"), sem("s_wah"), sem("s_was")
        s_xb = sem("s_xb")
        s_hi, s_lo = sem("s_hi"), sem("s_lo")
        s_t, s_xt = sem("s_t"), sem("s_xt")
        s_w, s_ph, s_c = sem("s_w"), sem("s_ph"), sem("s_c")
        s_acc, s_sum = sem("s_acc"), sem("s_sum")
        s_deg, s_degp, s_dis, s_disw = sem("s_deg"), sem("s_degp"), sem("s_dis"), sem("s_disw")
        s_u, s_v, s_h = sem("s_u"), sem("s_v"), sem("s_h")
        s_stat, s_aggr, s_ve, s_rstd, s_norm = (sem(n) for n in ("s_stat", "s_aggr", "s_ve", "s_rstd", "s_norm"))
        s_dmx, s_dmb, s_bias, s_gb, s_bw, s_bh, s_bl = (sem(n) for n in (
            "s_dmx", "s_dmb", "s_bias", "s_gb", "s_bw", "s_bh", "s_bl"))
        s_ht, s_yh, s_yl = sem("s_ht"), sem("s_yh"), sem("s_yl")
        s_srow = sem("s_srow")
        ld_rho = [sem(f"ld_rho{i}") for i in range(2)]
        s_rx, s_rho = sem("s_rx"), sem("s_rho")
        s_e, s_a, s_ah = sem("s_e"), sem("s_a"), sem("s_ah")
        s_al = [sem("s_al_dve"), sem("s_al_pool")]
        s_mm = sem("s_mm")
        s_z = sem("s_z")
        s_rd, s_ev = sem("s_rd"), sem("s_ev")
        s_out = sem("s_out")

        def tiles(eng, lo, hi, body):
            t = lo
            while t % R and t < hi:
                body(t, t % R)
                t += 1
            if hi - t > R:
                with eng.Fori(t // R, hi // R) as r:
                    for u in range(R):
                        body(r * R + u, u)
            else:
                for u in range(t, hi):
                    body(u, u % R)

        def pairs(eng, body, after):
            body(0, 0)
            with eng.Fori(0, PAIRS // 2 - 1) as c:
                body(c * 2 + 1, 1)
                body(c * 2 + 2, 0)
            body(PAIRS - 1, 1)
            after(PAIRS - 1)

        at = bass.ds
        block = ctx.enter_context(nc.Block())

        @block.sync
        def _(sp):
            xr = x_in.rearrange("(t p) d -> p t d", p=P)
            for r in range(R):
                sp.dma_start(x[:, r * R:(r + 1) * R, :], xr[:, r * R:(r + 1) * R, :]).then_inc(ld_x[r], 16)
            adj_n = adj_in.rearrange("c h p w -> (c h) p w")
            for s in range(STAGES):
                sp.dma_start(stage[:, s, :], adj_n[s]).then_inc(ld_adj[s], 16)
            with sp.Fori(1, NL // STAGES) as r:
                for s in range(STAGES):
                    sp.wait_ge(s_cast, r * STAGES + (s - STAGES + 1))
                    sp.dma_start(stage[:, s, :], adj_n[at(r * STAGES + s, 1)].rearrange("a p w -> p (a w)"))\
                      .then_inc(ld_adj[s], 16)
            sp.wait_ge(s_ph, 2 * T)
            sp.dma_start(s_dram, srow).then_inc(s_srow, 16)
            sp.wait_ge(s_srow, 16)

            def load_rho(chunk, b):
                for hh in range(2):
                    sp.dma_start(rho[:, b, hh, :], s_dram[2 * b + hh:2 * b + hh + 1, at(chunk * CH, CH)]
                                 .partition_broadcast(P)).then_inc(ld_rho[b], 16)

            load_rho(0, 0)
            load_rho(0, 1)
            with sp.Fori(1, N // CH) as c:
                for b in range(2):
                    sp.wait_ge(s_a, c * (2 * T) + (b - 1) * T)
                    load_rho(c, b)

            def store(t, u):
                sp.wait_ge(s_norm, t + (3 * T + 1))
                sp.dma_start(out.rearrange("(t p) d -> t p d", p=P)[at(t, 1)].rearrange("a p d -> p (a d)"),
                             x[:, at(t, 1), :].rearrange("p a d -> p (a d)")).then_inc(s_out, 16)
            tiles(sp, 0, T, store)
            sp.wait_ge(s_out, 16 * T)

        prep_w = {0: w0, 2: w2a, 3: w2b, 4: w3}

        def tile_of(buf, t):
            return buf[:, at(t, 1), :].rearrange("p a f -> p (a f)")

        @block.scalar
        def _(act):
            act.dma_start(w0f, w0_in.rearrange("(k p) h e -> p k (h e)", p=P)).then_inc(ld_w0, 16)
            act.dma_start(bias0, b0_in.rearrange("(a n) -> a n", a=1).partition_broadcast(P)).then_inc(ld_b, 16)
            act.dma_start(w1f, w1_in.rearrange("(k p) (h f) -> p k h f", p=P, h=H)).then_inc(ld_w1, 16)
            act.dma_start(abc.rearrange("p h s f -> p (h s f)"),
                          a_in.rearrange("h f a -> (f a) h").rearrange("f h -> h f").rearrange("(b h) f -> b (h f)", b=1)
                          .partition_broadcast(P)).then_inc(ld_a, 16)
            act.dma_start(part(r_flat, (0, 4 * D), F32, "p (c f) -> p c f", c=4),
                          w2a_in.rearrange("(c p) f -> p c f", p=P)).then_inc(ld_w2a, 16)
            act.dma_start(part(r_flat, (4 * D, 8 * D), F32, "p (c f) -> p c f", c=4),
                          w2b_in.rearrange("(c p) f -> p c f", p=P)).then_inc(ld_w2b, 16)
            act.dma_start(w3f, w3_in.rearrange("(k p) f -> p k f", p=P)).then_inc(ld_w3, 16)

            act.wait_ge(ld_w0, 16)
            nc.scalar.activation(w0[:, 0, :, :], w0f, ACT.Copy, scale=WS).then_inc(s_wh, 1)

            def split_hi(k, t, u, src, ready):
                ready(act)
                if not (k == 0 and isinstance(t, int) and t < R):
                    act.wait_ge(s_t, t + (k * T - R + 1))
                nc.scalar.activation(xs[:, u, 0, :], tile_of(src, t), ACT.Copy).then_inc(s_hi, 1)

            def take_t(k, t, u):
                act.wait_ge(s_t, t + (k * T + 1))
                nc.scalar.activation(tile_of(xt, t), tbank[u % 2], ACT.Copy).then_inc(s_xt, 1)

            def take_p(k, t, u):
                act.wait_ge(s_w, t + (k * T + 1))
                b = ps[:, 6 + u % 2, :]
                if k == 1:
                    nc.scalar.activation(srow[:, at(t * P, P)], b[0:H, P:2 * P], ACT.Copy, scale=1 / WS)\
                      .then_inc(s_ph, 1)
                    return
                dst = pset[k % 2][:, at(t, 1), 0, 0:D].rearrange("p a f -> p (a f)")
                src = b[:, D:2 * D] if k in (2, 3) else b[:, 0:D]
                nc.scalar.activation(dst, src, ACT.Copy, scale=disw[:, at(t, 1)] if k == 4 else 1 / WS)\
                  .then_inc(s_ph, 1)

            def joint(k, src, ready):
                for t in range(AHEAD):
                    split_hi(k, t, t, src, lambda e: ready(e, t))
                for t in range(1 + AHEAD - 1, T + AHEAD + 1):
                    if t < T:
                        split_hi(k, t, t % R, src, lambda e: ready(e, t))
                    if t - AHEAD < T:
                        take_t(k, t - AHEAD, (t - AHEAD) % R)
                    if t - AHEAD > 0:
                        take_p(k, t - AHEAD - 1, (t - AHEAD - 1) % R)

            def lagged(k, src, ready):
                for t in range(R):
                    split_hi(k, t, t, src, lambda e: ready(e, t))

                def one(t, u):
                    take_t(k, t - R, u)
                    take_p(k, t - R, u)
                    split_hi(k, t, u, src, lambda e: ready(e, t))
                tiles(act, R, T, one)
                for t in range(T - R, T):
                    take_t(k, t, t % R)
                    take_p(k, t, t % R)

            joint(0, x, lambda e, t: e.wait_ge(ld_x[t // R], 16))
            act.wait_ge(s_w, T)
            for n, bi in enumerate((b1_in, b2_in)):
                act.dma_start(b12[:, n, :], bi.rearrange("(a n) -> a n", a=1).partition_broadcast(P)).then_inc(ld_b12, 16)
            act.wait_ge(s_wa, 2 * K2)
            nc.scalar.activation(was[:, 0], wa[:, :, :, :], ACT.Copy, scale=WS).then_inc(s_wah, 1)
            for buf, src, s in ((w2a, w2af, ld_w2a), (w2b, w2bf, ld_w2b)):
                act.wait_ge(s, 16)
                nc.scalar.activation(buf[:, 0, :, :].rearrange("p k (s f) -> p k s f", s=2), src, ACT.Copy, scale=WS)\
                  .then_inc(s_wh, 1)
            act.wait_ge(ld_w1, 16)
            nc.scalar.activation(w1[:, 0, :, :], w1f.rearrange("p k h f -> p k (h f)"), ACT.Copy, scale=WS).then_inc(s_wh, 1)
            act.wait_ge(ld_w3, 16)
            nc.scalar.activation(w3[:, 0, :, :], w3f, ACT.Copy, scale=WS).then_inc(s_wh, 1)

            act.wait_ge(s_wl, 3)
            lagged(1, x, lambda e, t: e.wait_ge(s_norm, t + 1))

            act.wait_ge(s_bias, 2)
            for h in range(H):
                nc.scalar.activation(bet[:, h, :], dall[:, :, h], ACT.Exp, scale=SLOPE, bias=bias_b[:, h:h + 1])\
                  .then_inc(s_gb, 1)
            for h in range(H):
                nc.scalar.activation(gam[:, h, :], dall[:, :, h], ACT.Exp, scale=1 - SLOPE, bias=bias_g[:, h:h + 1])\
                  .then_inc(s_gb, 1)

            def rho_exp(p, b):
                chunk16 = p // 2 if isinstance(p, int) else None
                act.wait_ge(ld_rho[b], 32 * (chunk16 + 1) if chunk16 is not None else (p + (2 - b)) * 16)
                if isinstance(p, int) and p < 2:
                    pass
                for hh in range(2):
                    h = 2 * b + hh
                    ins = nc.scalar.activation(rho[:, b, hh, :], rho[:, b, hh, :], ACT.Exp, scale=-(1 - SLOPE),
                                               bias=bias_g[:, h:h + 1])
                ins.then_inc(s_rx, 1)

            act.wait_ge(s_bw, 1)

            def value_hi(t, u):
                for half in range(2):
                    act.wait_ge(s_ht, t * 2 + (half + 1))
                    for hh in range(2):
                        h = 2 * half + hh
                        ins = nc.scalar.activation(
                            val[0][:, at(t, 1), h, 0:D].rearrange("p a f -> p (a f)"),
                            ps[:, 2 * u + half, hh * D:(hh + 1) * D], ACT.Copy, scale=betw[:, h, at(t, 1)])
                    ins.then_inc(s_yh, 1)
            tiles(act, 0, T - R, value_hi)
            rho_exp(0, 0)

            def exp_adj(p, q, jt):
                chunk = (p - q) // 2 if isinstance(p, int) else None
                n = p * T + jt
                if not isinstance(n, int) or n >= 2:
                    act.wait_ge(s_a, n - 1)
                col = chunk * CH if chunk is not None else (p - q) * (CH // 2)
                nc.scalar.activation(ring_e[:, jt % 2, :], adj[:, jt, at(col, CH)], ACT.Exp).then_inc(s_e, 1)

            def att_hi(p, jt):
                act.wait_ge(s_a, p * T + (jt + 1))
                if jt > 3:
                    act.wait_ge(s_mm, p * (T - 1) + (jt - 3))
                elif isinstance(p, int) and p == 0:
                    act.wait_ge(s_ht, 2 * R * (jt + 1))
                elif jt == 3:
                    act.wait_ge(s_z, p * (2 * R))
                else:
                    act.wait_ge(s_mm, p * (T - 1) + (jt - 2))
                nc.scalar.activation(ring_hl[:, jt % 4, 0], ring_a[:, jt % 2], ACT.Copy).then_inc(s_ah, 1)

            exp_adj(0, 0, 0)
            exp_adj(0, 0, 1)
            att_hi(0, 0)
            tiles(act, T - R, T, value_hi)

            def pair(p, q):
                for jt in range(T):
                    if isinstance(p, int) and p == 0 and jt < 2:
                        continue
                    exp_adj(p, q, jt)
                    if jt > 0:
                        att_hi(p, jt - 1)
                    elif not isinstance(p, int) or p > 0:
                        att_hi(p - 1, T - 1)
                    if jt == 8 and not (isinstance(p, int) and p == PAIRS - 1):
                        rho_exp(p + 1, 1 - q)
            pairs(act, pair, lambda p: att_hi(p, T - 1))

            act.wait_ge(s_al[0], STEPS // 2)
            act.wait_ge(s_al[1], STEPS // 2)
            joint(2, x, lambda e, t: e.wait_ge(s_norm, t + (T + 1)))
            lagged(3, hid, lambda e, t: e.wait_ge(s_h, t + 1))
            lagged(4, x, lambda e, t: e.wait_ge(s_norm, t + (2 * T + 1)))

        @block.tensor
        def _(pe):
            def transpose(k, t, u):
                pe.wait_ge(s_lo, t + (k * T + 1))
                if not (isinstance(t, int) and k == 0 and t < 2):
                    pe.wait_ge(s_xt, t + (k * T - 1))
                for c in range(2 * K2):
                    ins = nc.tensor.transpose(tbank[u % 2][:, c * P:(c + 1) * P],
                                              xs[:, u, c // K2, (c % K2) * P:(c % K2 + 1) * P], ident[:, :])
                ins.then_inc(s_t, 1)

            TERMS = [(0, 0), (0, 1), (1, 0)]

            def project(k, t, u):
                pe.wait_ge(s_xt, t + (k * T + 1))
                if not (isinstance(t, int) and k == 0 and t < 2):
                    pe.wait_ge(s_c, t + (k * T - 1))
                if k == 2 and isinstance(t, int) and t < 2:
                    pe.wait_ge(s_ev, 2 * R * (PAIRS - 1) + 7 + t)
                xtt = tile_of(xt, t)
                bank = ps[:, 6 + u % 2, :]

                def xpart(a, kk):
                    return xtt[:, (a * K2 + kk) * P:(a * K2 + kk + 1) * P]
                steps = [(a, b, kk) for kk in range(K2) for a, b in TERMS]
                if k == 1:
                    for n, (a, b, kk) in enumerate(steps):
                        nc.tensor.matmul(bank[:, 0:H], xpart(a, kk), was[:, b, kk, 1, :],
                                         start=(n == 0), stop=(n == len(steps) - 1))
                    for n, (a, b, kk) in enumerate(steps):
                        ins = nc.tensor.matmul(bank[0:H, P:2 * P], was[:, b, kk, 0, :], xpart(a, kk),
                                               start=(n == 0), stop=(n == len(steps) - 1))
                    ins.then_inc(s_w, 1)
                    return
                w = prep_w[k]
                width = w.shape[3]
                for n, (a, b, kk) in enumerate(steps):
                    ins = nc.tensor.matmul(bank[:, 0:width], xpart(a, kk), w[:, b, kk, :],
                                           start=(n == 0), stop=(n == len(steps) - 1))
                ins.then_inc(s_w, 1)

            def agg_step(a, k, it, bank, j, done):
                width = D + 1 if a == 0 else D
                pp = pset[k % 2]
                lhs = adj[:, j, at(it * P, P)]
                nc.tensor.matmul(ps[:, bank, 0:width], lhs, pp[:, j, 0, 0:width], start=(j == 0), stop=False)
                ins = nc.tensor.matmul(ps[:, bank, 0:D], lhs, pp[:, j, 1, 0:D], start=False, stop=(j == T - 1))
                if done:
                    ins.then_inc(s_acc, 1)

            def group0(a, k, js):
                for j in js:
                    pe.wait_ge(s_c, k * T + j + 1)
                    for it in range(R):
                        if j == 0 and a > 0:
                            pe.wait_ge(s_sum, (a - 1) * T + T - R + it + 1)
                        agg_step(a, k, it, it, j, j == T - 1)

            def joint(k, a, before_agg):
                transpose(k, 0, 0)
                for t in range(T):
                    if t + 1 < T:
                        transpose(k, t + 1, (t + 1) % R)
                    project(k, t, t % R)
                    if t == T // 2:
                        before_agg()
                    if t >= T // 2:
                        j0 = 2 * (t - T // 2)
                        group0(a, k, [j for j in (j0 - 1, j0) if j >= 0])
                group0(a, k, [T - 1])

            def rest(a, knext, ready):
                k = (0, 2, 3, 4)[a]

                def one(t, u):
                    ready(t, u)
                    pe.wait_ge(s_sum, t + (a * T - R + 1))
                    for j in range(T):
                        if j == T // 2 + 2 and knext is not None:
                            transpose(knext, t - R, u)
                        agg_step(a, k, t, u, j, j == T - 1)
                    if knext is not None:
                        project(knext, t - R, u)
                tiles(pe, R, T, one)

            def tail(k, a):
                e = T - R
                plan = [([0, 1, 2, 3], e, None), ([4, 5], e + 1, e), ([6, 7], e + 2, e + 1),
                        ([8, 9], e + 3, e + 2), ([10, 11], None, e + 3), (list(range(e, T)), None, None)]
                for js, tt, tp in plan:
                    group0(a, k, js)
                    if tt is not None:
                        transpose(k, tt, tt % R)
                    if tp is not None:
                        project(k, tp, tp % R)

            pe.wait_ge(s_id, 1)
            pe.wait_ge(s_wl, 1)
            joint(0, 0, lambda: (pe.wait_ge(s_cast, 4), pe.wait_ge(s_one, 1)))

            def cast_ready(t, u):
                pe.wait_ge(s_cast, t + 2 if u % 2 == 0 else t + 1)
            pe.wait_ge(s_was, 1)
            rest(0, 1, cast_ready)

            def values(t, u):
                xtt = tile_of(xt, t)
                for half in range(2):
                    if not (isinstance(t, int) and t < R):
                        pe.wait_ge(s_yl, t * 2 + (half + 1 - 2 * R))
                    steps = [(a, b, kk) for kk in range(K2) for a, b in TERMS]
                    for n, (a, b, kk) in enumerate(steps):
                        ins = nc.tensor.matmul(ps[:, 2 * u + half, :],
                                               xtt[:, (a * K2 + kk) * P:(a * K2 + kk + 1) * P],
                                               w1[:, b, kk, half * 512:(half + 1) * 512],
                                               start=(n == 0), stop=(n == len(steps) - 1))
                    ins.then_inc(s_ht, 1)
            for t in range(T - R, T):
                transpose(1, t, t % R)
                project(1, t, t % R)
                if t == T - 3:
                    pe.wait_ge(s_wl, 5)
                    pe.wait_ge(s_sum, T - 2)
                    values(0, 0)
                if t == T - 2:
                    pe.wait_ge(s_sum, T)
                    values(1, 1)
            pe.wait_ge(s_xt, 2 * T)
            values(2, 2)
            pe.wait_ge(s_c, 2 * T)
            values(3, 3)
            tiles(pe, R, T, values)

            pe.wait_ge(s_bl, 1)

            def pair(p, q):
                first = isinstance(p, int) and p == 0
                for jt in range(T):
                    pe.wait_ge(s_al[jt % 2], p * (T // 2) + (jt // 2 + 1))
                    for b in range(2 * R):
                        hh, it = b // R, b % R
                        if jt == 0 and first:
                            pe.wait_ge(s_yl, 2 * T - 2 * R + b + 1)
                        if jt == 0 and not first:
                            pe.wait_ge(s_ev, p * (2 * R) + (b + 1 - 2 * R))
                        h = 2 * q + hh
                        hi = ring_hl[:, jt % 4, 0, hh, it * P:(it + 1) * P]
                        lo = ring_hl[:, jt % 4, 1, hh, it * P:(it + 1) * P]
                        acc = ps[:, b, 0:D + 1]
                        nc.tensor.matmul(acc, hi, val[0][:, jt, h, 0:D + 1], start=(jt == 0), stop=False)
                        nc.tensor.matmul(acc, hi, val[1][:, jt, h, 0:D + 1], start=False, stop=False)
                        ins = nc.tensor.matmul(acc, lo, val[0][:, jt, h, 0:D + 1], start=False, stop=(jt == T - 1))
                        if jt == T - 1:
                            ins.then_inc(s_z, 1)
                    if jt < T - 1:
                        ins.then_inc(s_mm, 1)
            pairs(pe, pair, lambda p: None)

            pe.wait_ge(s_ev, 2 * R * (PAIRS - 1) + 6)
            joint(2, 1, lambda: None)
            rest(1, 3, lambda t, u: None)
            tail(3, 2)
            rest(2, 4, lambda t, u: None)
            tail(4, 3)
            rest(3, None, lambda t, u: None)

        @block.vector
        def _(dve):
            dve.wait_ge(s_wh, 1)
            nc.vector.scalar_tensor_tensor(w0[:, 1, :, :], w0f, WS, w0[:, 0, :, :], op0=ALU.mult, op1=ALU.subtract)\
              .then_inc(s_wl, 1)

            def cast(n, s, r):
                dve.wait_ge(ld_adj[s], r * 16)
                src = stage[:, s, :].rearrange("p (j w) -> p j w", j=JH)
                nc.vector.tensor_copy(adj[:, (s % 2) * JH:(s % 2 + 1) * JH, at(n, LW)], src).then_inc(s_cast, 1)

            def cast_n(n):
                cast((n // 2) * LW, n % STAGES, n // STAGES + 1)

            def split_lo(k, t, u, src):
                dve.wait_ge(s_hi, t + (k * T + 1))
                nc.vector.tensor_sub(xs[:, u, 1, :], tile_of(src, t), xs[:, u, 0, :]).then_inc(s_lo, 1)

            def take(k, t, u):
                dve.wait_ge(s_ph, t + (k * T + 1))
                b = ps[:, 6 + u % 2, :]
                if k == 1:
                    nc.vector.tensor_scalar(tile_of(dall, t), b[:, 0:H], 1 / WS, None, ALU.mult).then_inc(s_c, 1)
                    return
                hi = pset[k % 2][:, at(t, 1), 0, 0:D].rearrange("p a f -> p (a f)")
                lo = pset[k % 2][:, at(t, 1), 1, 0:D].rearrange("p a f -> p (a f)")
                ot = tile_of(own, t)
                if k in (2, 3):
                    nc.vector.scalar_tensor_tensor(ot, b[:, 0:D], 1 / WS, b12[:, k - 2, :],
                                                   op0=ALU.mult, op1=ALU.add)
                if k == 4:
                    nc.vector.tensor_scalar(ot, b[:, 0:D], disw[:, at(t, 1)], None, ALU.mult)
                src = b[:, D:2 * D] if k in (2, 3) else b[:, 0:D]
                nc.vector.scalar_tensor_tensor(lo, src, disw[:, at(t, 1)] if k == 4 else 1 / WS, hi,
                                               op0=ALU.mult, op1=ALU.subtract).then_inc(s_c, 1)

            def hold(s, value):
                dve.wait_ge(s, value)
                nc.vector.memset(held[:, :], 0.0)

            def statistics(l, slot):
                nc.vector.bn_stats(stat[:, slot, :], total[:, slot, :]).then_inc(s_stat, 1)
                hold(s_stat, l + 1)
                nc.vector.bn_aggr(mv[:, slot, :], stat[:, slot, :]).then_inc(s_aggr, 1)

            def normalise(l, slot, xt_):
                dve.wait_ge(s_rstd, l + 1)
                nc.vector.tensor_scalar(xt_, total[:, slot, :], mv[:, slot, 0:1], rstd[:, slot:slot + 1],
                                        ALU.subtract, ALU.mult).then_inc(s_norm, 1)

            def stages(a, k, t, u):
                q, l = t + a * T, t + (a - 2) * T
                acc, xt_, ot, ht_, tot = ps[:, u, 0:D], tile_of(x, t), tile_of(own, t), tile_of(hid, t), total[:, u, :]

                def first():
                    if a == 0 and isinstance(t, int) and t == 0:
                        dve.wait_ge(s_xb, T)
                    dve.wait_ge(s_acc, q + 1)
                    if a == 0:
                        nc.vector.tensor_copy(deg[:, at(t, 1)], ps[:, u, D:D + 1]).then_inc(s_deg, 1)
                        nc.vector.tensor_tensor(tot, acc, xt_, ALU.add).then_inc(s_sum, 1)
                    else:
                        nc.vector.tensor_tensor(ht_ if a == 1 else ot, acc, ot, ALU.add).then_inc(s_sum, 1)

                def relu():
                    dve.wait_ge(s_sum, q + 1)
                    if a == 1:
                        nc.vector.tensor_scalar(ht_, ht_, 0.0, None, ALU.max).then_inc(s_h, 1)
                    elif a == 2:
                        nc.vector.scalar_tensor_tensor(ot, ot, 0.0, ht_, op0=ALU.max, op1=ALU.add).then_inc(s_u, 1)
                    else:
                        nc.vector.tensor_scalar(ot, ot, dis[:, at(t, 1)], 0.0, ALU.mult, ALU.max).then_inc(s_u, 1)

                def residual():
                    dve.wait_ge(s_u, l + 1)
                    if a == 2:
                        nc.vector.scalar_tensor_tensor(tot, ot, 0.0, xt_, op0=ALU.max, op1=ALU.add).then_inc(s_v, 1)
                    else:
                        nc.vector.tensor_tensor(tot, ot, xt_, ALU.add).then_inc(s_v, 1)

                def stats():
                    if a == 0:
                        dve.wait_ge(s_sum, q + 1)
                    else:
                        dve.wait_ge(s_v, l + 1)
                    nc.vector.bn_stats(stat[:, u, :], tot).then_inc(s_stat, 1)

                def aggregate_stats():
                    hold(s_stat, q + 1)
                    nc.vector.bn_aggr(mv[:, u, :], stat[:, u, :]).then_inc(s_aggr, 1)

                out_ = [first]
                if a > 0:
                    out_.append(relu)
                if a > 1:
                    out_.append(residual)
                if a != 1:
                    out_ += [stats, aggregate_stats]
                late_ = [lambda: normalise(q, u, xt_)] if a != 1 else []
                if k is not None:
                    late_.append(lambda: split_lo(k, t, u, hid if a == 1 else x))
                return out_, late_

            def aggregate(a, k, extra=lambda t: None):
                lines = [sum(stages(a, k, t, t), []) for t in range(R)]
                for line in lines:
                    line[0]()
                for s in range(1, len(lines[0]) + R - 1):
                    for t in range(R):
                        if 1 <= s - t < len(lines[t]):
                            lines[t][s - t]()

                def one(t, u):
                    if isinstance(t, int):
                        extra(t)
                    early, late_ = stages(a, k, t, u)
                    for st in early:
                        st()
                    if k is not None:
                        take(k, t - R, u)
                    for st in late_:
                        st()
                if a == 0:
                    for t in range(R, 2 * R):
                        one(t, t % R)
                    tiles(dve, 2 * R, T, one)
                else:
                    tiles(dve, R, T, one)
                if k is not None:
                    for t in range(T - R, T):
                        take(k, t, t % R)

            CASTS_AT = {5: 0, 6: 1, 8: 2, 9: 3, 11: 4, 13: 5, 15: 6}
            for t in range(T + AHEAD + 1):
                if t < T:
                    dve.wait_ge(ld_x[t // R], 16)
                    split_lo(0, t, t % R, x)
                if t > AHEAD:
                    take(0, t - AHEAD - 1, (t - AHEAD - 1) % R)
                if t - AHEAD in CASTS_AT:
                    cast_n(CASTS_AT[t - AHEAD])
                if t - AHEAD in (8, 10, 12, 14):
                    n = (t - AHEAD - 8) // 2
                    dve.wait_ge(s_prod, n + 1)
                    nc.vector.reduce_sum(wa[:, n // 2, n % 2, :], prod, axis=AX.X).then_inc(s_wa, 1)

            def weight_lo(n, buf, src):
                dve.wait_ge(s_wh, n + 1)
                for kk in range(K2):
                    hi, lo = buf[:, 0, kk, :], buf[:, 1, kk, :]
                    if n in (1, 2):
                        hi, lo = (v.rearrange("p (s f) -> p s f", s=2) for v in (hi, lo))
                    ins = nc.vector.scalar_tensor_tensor(lo, src[:, kk], WS, hi, op0=ALU.mult, op1=ALU.subtract)
                ins.then_inc(s_wl, 1)

            cast_n(7)
            dve.wait_ge(s_wah, 1)
            nc.vector.scalar_tensor_tensor(was[:, 1], wa[:, :, :, :], WS, was[:, 0], op0=ALU.mult, op1=ALU.subtract)\
              .then_inc(s_was, 1)
            weight_lo(1, w2a, w2af)
            cast_n(8)
            weight_lo(2, w2b, w2bf)
            cast_n(9)
            cast_n(10)

            def late(t):
                if t == R:
                    cast_n(11)
                if t == R + 1:
                    cast_n(12)
                    cast_n(13)
                if t == R + 2:
                    cast_n(14)
                    cast_n(15)
                if t == R + 3:
                    weight_lo(3, w1, w1f.rearrange("p k h f -> p k (h f)"))
                    weight_lo(4, w3, w3f)
            aggregate(0, 1, late)

            dve.wait_ge(s_c, 2 * T)
            nc.vector.reduce_max(dmx[:, :], dall[:, :, :].rearrange("p t h -> p h t"), axis=AX.X).then_inc(s_dmx, 1)
            dve.wait_ge(s_dmb, 1)
            nc.vector.tensor_scalar(bias_b[:, :], dmb[:, :], -SLOPE, None, ALU.mult).then_inc(s_bias, 1)
            nc.vector.tensor_scalar(bias_g[:, :], dmb[:, :], -(1 - SLOPE), LCAP, ALU.mult, ALU.add).then_inc(s_bias, 1)
            dve.wait_ge(s_gb, H)
            nc.vector.tensor_scalar(betw[:, :, :], bet[:, :, :], 1 / WS, None, ALU.mult).then_inc(s_bw, 1)
            nc.vector.tensor_scalar(bet4[:, :, :], bet[:, :, :], float(H), None, ALU.mult).then_inc(s_bw, 1)
            dve.wait_ge(s_bw, 2)

            def value_lo(t, u):
                for half in range(2):
                    dve.wait_ge(s_yh, t * 2 + (half + 1))
                    for hh in range(2):
                        h = 2 * half + hh
                        ins = nc.vector.scalar_tensor_tensor(
                            val[1][:, at(t, 1), h, 0:D].rearrange("p a f -> p (a f)"),
                            ps[:, 2 * u + half, hh * D:(hh + 1) * D], betw[:, h, at(t, 1)],
                            val[0][:, at(t, 1), h, 0:D].rearrange("p a f -> p (a f)"),
                            op0=ALU.mult, op1=ALU.subtract)
                    ins.then_inc(s_yl, 1)
            value_lo(0, 0)
            b4 = bet4[:, :, :].rearrange("p h t -> p t h")
            nc.vector.tensor_copy(val[0][:, :, :, D], b4).then_inc(s_bh, 1)
            dve.wait_ge(s_bh, 1)
            nc.vector.tensor_tensor(val[1][:, :, :, D], b4, val[0][:, :, :, D], ALU.subtract).then_inc(s_bl, 1)
            for t in range(1, R):
                value_lo(t, t)
            tiles(dve, R, T - R, value_lo)
            dve.wait_ge(s_gb, 2 * H)

            def cap_rho(p, b):
                dve.wait_ge(s_rx, p + 1)
                nc.vector.tensor_scalar(rho[:, b], rho[:, b], math.exp(LCAP), None, ALU.min).then_inc(s_rho, 1)
            cap_rho(0, 0)

            def weights(p, q, jt):
                n = p * T + jt
                if jt == 0:
                    dve.wait_ge(s_rho, p + 1)
                dve.wait_ge(s_e, n + 1)
                if not isinstance(n, int) or n >= 2:
                    dve.wait_ge(s_ah, n - 1)
                    dve.wait_ge(s_al[jt % 2], p * (T // 2) + jt // 2)
                for hh in range(2):
                    h = 2 * q + hh
                    ins = nc.vector.scalar_tensor_tensor(
                        ring_a[:, jt % 2, hh, :], rho[:, q, hh, :], gam[:, h, jt:jt + 1], ring_e[:, jt % 2, :],
                        op0=ALU.max, op1=ALU.mult)
                ins.then_inc(s_a, 1)

            def att_lo(m, jt):
                dve.wait_ge(s_ah, m + 1)
                nc.vector.tensor_sub(ring_hl[:, jt % 4, 1], ring_a[:, jt % 2], ring_hl[:, jt % 4, 0])\
                  .then_inc(s_al[0], 1)

            weights(0, 0, 0)
            weights(0, 0, 1)
            att_lo(0, 0)
            tiles(dve, T - R, T, value_lo)

            def take_attention(p, q):
                first = (p - q) * 2
                for b in range(2 * R + 1):
                    if b < 2 * R:
                        dve.wait_ge(s_z, p * (2 * R) + (b + 1))
                        nc.vector.reciprocal(rden[:, b:b + 1], ps[:, b, D:D + 1]).then_inc(s_rd, 1)
                    if b == 0:
                        continue
                    b -= 1
                    it = b % R
                    dve.wait_ge(s_rd, p * (2 * R) + (b + 1))
                    if b >= R:
                        dve.wait_ge(s_ev, p * (2 * R) + (it + 1))
                    xt_ = tile_of(x, first + it)
                    dst = total[:, it, :] if q == 1 and b >= R else xt_
                    nc.vector.scalar_tensor_tensor(dst, ps[:, b, 0:D], rden[:, b:b + 1], xt_,
                                                   op0=ALU.mult, op1=ALU.add).then_inc(s_ev, 1)

            def chunk_statistics(p):
                first = (p - 1) * 2
                dve.wait_ge(s_ev, p * (2 * R) + 2 * R)
                for it in range(R):
                    statistics(first + (T + it), it)

            def chunk_normalise(p):
                first = (p - 1) * 2
                for it in range(R):
                    normalise(first + (T + it), it, tile_of(x, first + it))

            def pair(p, q):
                first = isinstance(p, int) and p == 0
                for jt in range(T):
                    if not (first and jt < 2):
                        weights(p, q, jt)
                        if jt % 2 == 1:
                            att_lo(p * T + (jt - 1), jt - 1)
                    if not first:
                        if jt == 2:
                            take_attention(p - 1, 1 - q)
                        if q == 0 and jt == 5:
                            chunk_statistics(p - 1)
                        if q == 0 and jt == 8:
                            chunk_normalise(p - 1)
                    if jt == 12 and not (isinstance(p, int) and p == PAIRS - 1):
                        cap_rho(p + 1, 1 - q)

            def end(p):
                for t in range(AHEAD):
                    split_lo(2, t, t, x)
                take_attention(p, 1)
            pairs(dve, pair, end)

            dve.wait_ge(ld_b12, 32)
            for t in range(AHEAD, T + AHEAD + 1):
                if t < T:
                    split_lo(2, t, t % R, x)
                if t == AHEAD:
                    chunk_statistics(PAIRS - 1)
                if t == AHEAD + 1:
                    chunk_normalise(PAIRS - 1)
                if t > AHEAD:
                    take(2, t - AHEAD - 1, (t - AHEAD - 1) % R)
            aggregate(1, 3)
            aggregate(2, 4)
            aggregate(3, None)

        @block.gpsimd
        def _(pool):
            nc.gpsimd.memset(ident[:, :], 0.0).then_inc(s_id0, 1)
            nc.gpsimd.memset(pset[0][:, :, 0, D:D + 1], 1.0).then_inc(s_one, 1)
            pool.wait_ge(s_id0, 1)
            nc.gpsimd.affine_select(out=ident[:, :], in_=ident[:, :], compare_op=ALU.not_equal, fill=1.0, base=0,
                                    pattern=[[-1, P]], channel_multiplier=1).then_inc(s_id, 1)
            nc.gpsimd.memset(neghalf[:, :], -0.5).then_inc(s_nh, 1)
            nc.gpsimd.memset(epsv[:, :], EPS).then_inc(s_nh, 1)
            pool.wait_ge(s_nh, 2)
            pool.wait_ge(ld_w1, 16)
            pool.wait_ge(ld_a, 16)
            for n in range(2 * K2):
                if n:
                    pool.wait_ge(s_wa, n)
                nc.gpsimd.tensor_tensor(prod, w1f[:, n // 2], abc[:, :, n % 2, :], ALU.mult).then_inc(s_prod, 1)
            pool.wait_ge(ld_b, 16)

            def add_b0(t, u):
                pool.wait_ge(s_lo, t + 1)
                nc.gpsimd.tensor_tensor(tile_of(x, t), tile_of(x, t), bias0, ALU.add).then_inc(s_xb, 1)
            tiles(pool, 0, T, add_b0)

            def inv_std(l, slot):
                pool.wait_ge(s_aggr, l + 1)
                nc.gpsimd.tensor_tensor(veps[:, slot:slot + 1], mv[:, slot, 1:2], epsv[:, :], ALU.add).then_inc(s_ve, 1)
                pool.wait_ge(s_ve, l + 1)
                nc.gpsimd.tensor_tensor(rstd[:, slot:slot + 1], veps[:, slot:slot + 1], neghalf[:, 0:1], ALU.pow)\
                  .then_inc(s_rstd, 1)
            tiles(pool, 0, T, inv_std)
            pool.wait_ge(s_dmx, 1)
            nc.gpsimd.partition_all_reduce(dmb[:, :], dmx[:, :], P, bass.bass_isa.ReduceOp.max).then_inc(s_dmb, 1)
            pool.wait_ge(s_deg, T)
            nc.gpsimd.tensor_scalar(degp[:, :], deg[:, :], 1.0, None, ALU.add).then_inc(s_degp, 1)
            pool.wait_ge(s_degp, 1)
            nc.gpsimd.tensor_tensor(dis[:, :], degp[:, :], neghalf[:, :], ALU.pow).then_inc(s_dis, 1)
            pool.wait_ge(s_dis, 1)
            nc.gpsimd.tensor_scalar(disw[:, :], dis[:, :], 1 / WS, None, ALU.mult).then_inc(s_disw, 1)

            def att_lo(m, jt):
                pool.wait_ge(s_ah, m + 1)
                nc.gpsimd.tensor_sub(ring_hl[:, jt % 4, 1], ring_a[:, jt % 2], ring_hl[:, jt % 4, 0])\
                  .then_inc(s_al[1], 1)

            def pair(p, q):
                first = isinstance(p, int) and p == 0
                for jt in range(1, T, 2):
                    att_lo(p * T + jt, jt)
                    if jt == 5 and q == 0 and not first:
                        for it in range(R):
                            inv_std((p - 2) * 2 + (T + it), it)
            pairs(pool, pair, lambda p: [inv_std((p - 1) * 2 + (T + it), it) for it in range(R)])
            tiles(pool, 2 * T, 4 * T, inv_std)


_ORDER = ["x", "adj", "L0_gnn_W", "L0_gnn_b", "L1_gnn_W", "L1_gnn_a", "L2_gnn_W1", "L2_gnn_b1", "L2_gnn_W2",
          "L2_gnn_b2", "L3_gnn_W"]


def kernel(**inputs):
    import numpy as np
    import concourse.bacc as bacc
    from concourse import mybir as _mybir
    from concourse.bass_utils import run_bass_kernel_spmd

    host = {k: np.asarray(inputs[k]) for k in _ORDER}
    n = host["adj"].shape[0]
    blocks, halves, p = 8, 2, 128
    host["adj"] = np.ascontiguousarray(
        host["adj"].T.reshape(halves, n // (halves * p), p, blocks, n // blocks).transpose(3, 0, 2, 1, 4)
        .reshape(blocks, halves, p, -1))
    host["L0_gnn_W"] = np.ascontiguousarray(host["L0_gnn_W"].transpose(1, 0, 2))
    host["L0_gnn_b"] = host["L0_gnn_b"].reshape(-1)

    nc = bacc.Bacc("TRN2", target_bir_lowering=False, num_devices=1)
    arrays, args = {}, []
    for k in _ORDER:
        a = np.ascontiguousarray(host[k])
        arrays[f"in_{k}"] = a
        args.append(nc.dram_tensor(f"in_{k}", a.shape, _mybir.dt.from_np(a.dtype), kind="ExternalInput").ap())
    args.append(nc.dram_tensor("out_x", host["x"].shape, _mybir.dt.float32, kind="ExternalOutput").ap())
    graph_stack(nc, *args)
    r = run_bass_kernel_spmd(nc, [arrays], core_ids=[0])
    return r.results[0]["out_x"]
```

```python
import math
from contextlib import ExitStack

import concourse.bass as bass
from concourse import mybir


def graph_stack(nc, x_in, adj_in, w0_in, b0_in, w1_in, a_in, w2a_in, b1_in, w2b_in, b2_in, w3_in, out):
    F32, F16, BF16 = mybir.dt.float32, mybir.dt.float16, mybir.dt.bfloat16
    ALU, ACT, AX = mybir.AluOpType, mybir.ActivationFunctionType, mybir.AxisListType

    P = 128
    N, D = x_in.shape
    T = N // P
    H, A2 = a_in.shape[0], a_in.shape[1]
    K2 = D // P
    KI = 2 * K2 * P
    R = 4
    CH = R * P
    PAIRS = (N // CH) * (H // 2)
    STEPS = PAIRS * T
    PW = D + 2
    WS = 64.0
    LCAP = 6 * math.log(2.0)
    SLOPE = 0.01
    EPS = 1e-5
    AHEAD = 3
    NL = 16
    LW = N // (NL // 2)
    JH = T // 2
    FIRST_LOADS = (0, 2, 1, 3)
    FIRST_CASTS = 5

    ctx = ExitStack()
    with ctx:
        def sb(name, shape, dt):
            return ctx.enter_context(nc.sbuf_tensor(name, shape, dt))

        def sem(name):
            return ctx.enter_context(nc.semaphore(name))

        adj = sb("adj", [P, T, N], BF16)
        x = sb("x", [P, T, D], F32)
        arena = sb("arena", [P, 2 * T * H * PW // 2], F32)
        w0 = sb("w0", [P, 2, K2, D], F16)
        w1 = sb("w1", [P, 2, K2, H * D], F16)
        w2a = sb("w2a", [P, 2, K2, 2 * D], F16)
        w2b = sb("w2b", [P, 2, K2, 2 * D], F16)
        w3 = sb("w3", [P, 2, K2, D], F16)
        rho = sb("rho", [P, 2, 2, CH], F32)
        ring_e = sb("ring_e", [P, 2, CH], F32)
        ring_a = sb("ring_a", [P, 2, 2, CH], F32)
        ring_hl = sb("ring_hl", [P, 4, 2, 2, CH], F16)
        ident = sb("ident", [P, P], F16)
        stat = sb("stat", [P, R, 6], F32)
        mv = sb("mv", [P, R, 2], F32)
        veps = sb("veps", [P, R], F32)
        rstd = sb("rstd", [P, R], F32)
        epsv = sb("epsv", [P, 1], F32)
        held = sb("held", [P, 1], F32)
        total = sb("total", [P, R, D], F32)
        b12 = w0[:, :, :, :].rearrange("p a k f -> p (a k f)").bitcast(F32).rearrange("p (a f) -> p a f", a=2)
        bias0 = total[:, R - 1, :]
        neghalf = sb("neghalf", [P, T], F32)
        deg = sb("deg", [P, T], F32)
        degp = sb("degp", [P, T], F32)
        dis = sb("dis", [P, T], F32)
        disw = sb("disw", [P, T], F32)
        dis2w = sb("dis2w", [P, T], F32)
        wa = sb("wa", [P, K2, 2, H], F32)
        was = sb("was", [P, 2, K2, 2, H], F16)
        dall = sb("dall", [P, T, H], F32)
        dmx = sb("dmx", [P, H], F32)
        dmb = sb("dmb", [P, H], F32)
        bias_g = sb("bias_g", [P, H], F32)
        bias_b = sb("bias_b", [P, H], F32)
        gam = sb("gam", [P, H, T], F32)
        bet = sb("bet", [P, H, T], F32)
        betw = sb("betw", [P, H, T], F32)
        bet4 = sb("bet4", [P, H, T], F32)
        rden = sb("rden", [P, 2 * R], F32)
        ps = ctx.enter_context(nc.psum_tensor("ps", [P, 8, 512], F32))
        s_dram = nc.dram_tensor("s_scratch", [H, N], F32, kind="Internal").ap()

        def part(base, words, dt, text, **kw):
            v = base[:, words[0]:words[1]]
            if dt is not F32:
                v = v.bitcast(dt)
            return v.rearrange(text, **kw) if text else v

        PSET = T * 2 * PW // 2
        pset = [part(arena, (s * PSET, (s + 1) * PSET), F16, "p (t q f) -> p t q f", t=T, q=2) for s in range(2)]
        own = part(arena, (2 * PSET, 2 * PSET + T * D), F32, "p (t f) -> p t f", t=T)
        hid = part(arena, (2 * PSET + T * D, 2 * PSET + 2 * T * D), F32, "p (t f) -> p t f", t=T)
        STAGES = 4
        SW = JH * LW
        stage = part(arena, (PSET, PSET + STAGES * SW), F32, "p (s w) -> p s w", s=STAGES)
        w1f = part(arena, (PSET + STAGES * SW, PSET + STAGES * SW + K2 * H * D), F32, "p (k h f) -> p k h f", k=K2, h=H)
        o = PSET + STAGES * SW + K2 * H * D
        w1ff = w1f.rearrange("p k h f -> p k (h f)")
        abc = part(arena, (o, o + H * A2), F32, "p (h s f) -> p h s f", h=H, s=2)
        VW = T * H * PW // 2
        val = [part(arena, (s * VW, (s + 1) * VW), F16, "p (t h f) -> p t h f", t=T, h=H) for s in range(2)]
        a_flat = ring_a[:, :, :, :].rearrange("p a b c -> p (a b c)")
        xs = part(a_flat, (0, R * D), F16, "p (s q f) -> p s q f", s=R, q=2)
        w0f = part(a_flat, (R * D, R * D + K2 * D), F32, "p (k f) -> p k f", k=K2)
        w3f = part(a_flat, (R * D + K2 * D, R * D + 2 * K2 * D), F32, "p (k f) -> p k f", k=K2)
        r_flat = rho[:, :, :, :].rearrange("p a b c -> p (a b c)")
        w2af = part(r_flat, (0, 4 * D), F32, "p (s k f) -> p k s f", s=2, k=K2)
        w2bf = part(r_flat, (4 * D, 8 * D), F32, "p (s k f) -> p k s f", s=2, k=K2)
        srow = r_flat[0:H, :]
        prod = ring_e[:, :, :].rearrange("p a (h f) -> p (a h) f", f=D)
        xt = ring_hl[:, :, :, :, :].rearrange("p a b c d -> p (a b c d)").rearrange("p (t c) -> p t c", t=T)
        tbank = [ps[:, 4 + b, 0:KI // 2].bitcast(F16) for b in range(2)]

        ld_x = [sem(f"ld_x{i}") for i in range(R + 1)]
        ld_adj = [sem(f"ld_adj{i}") for i in range(STAGES)]
        ld_w0, ld_w3, ld_w1, ld_w2a, ld_w2b, ld_a, ld_b, ld_b12 = (sem(n) for n in (
            "ld_w0", "ld_w3", "ld_w1", "ld_w2a", "ld_w2b", "ld_a", "ld_b", "ld_b12"))
        s_cast, s_cast_act = sem("s_cast"), sem("s_cast_act")
        s_id0, s_id, s_one, s_nh = sem("s_id0"), sem("s_id"), sem("s_one"), sem("s_nh")
        s_wh, s_wl = sem("s_wh"), sem("s_wl")
        s_prod, s_wa, s_wah, s_was = sem("s_prod"), sem("s_wa"), sem("s_wah"), sem("s_was")
        s_xb = sem("s_xb")
        s_hi, s_lo = sem("s_hi"), sem("s_lo")
        s_t, s_xt = sem("s_t"), sem("s_xt")
        s_w, s_ph, s_c = sem("s_w"), sem("s_ph"), sem("s_c")
        s_acc, s_sum = sem("s_acc"), sem("s_sum")
        s_deg, s_degp, s_dis, s_disw = sem("s_deg"), sem("s_degp"), sem("s_dis"), sem("s_disw")
        s_u, s_v, s_h = sem("s_u"), sem("s_v"), sem("s_h")
        s_stat, s_aggr, s_ve, s_rstd, s_norm = (sem(n) for n in ("s_stat", "s_aggr", "s_ve", "s_rstd", "s_norm"))
        s_dmx, s_dmb, s_bias, s_gb, s_bw, s_bh, s_bl = (sem(n) for n in (
            "s_dmx", "s_dmb", "s_bias", "s_gb", "s_bw", "s_bh", "s_bl"))
        s_ht, s_yh, s_yl = sem("s_ht"), sem("s_yh"), sem("s_yl")
        s_srow = sem("s_srow")
        ld_rho = [sem(f"ld_rho{i}") for i in range(2)]
        s_rx, s_rho = sem("s_rx"), sem("s_rho")
        s_e, s_a, s_ah = sem("s_e"), sem("s_a"), sem("s_ah")
        s_al = [sem("s_al_dve"), sem("s_al_pool")]
        s_mm = sem("s_mm")
        s_z = sem("s_z")
        s_rd, s_ev = sem("s_rd"), sem("s_ev")
        s_out = sem("s_out")

        def tiles(eng, lo, hi, body):
            t = lo
            while t % R and t < hi:
                body(t, t % R)
                t += 1
            if hi - t > R:
                with eng.Fori(t // R, hi // R) as r:
                    for u in range(R):
                        body(r * R + u, u)
            else:
                for u in range(t, hi):
                    body(u, u % R)

        def pairs(eng, body, after):
            body(0, 0)
            with eng.Fori(0, PAIRS // 2 - 1) as c:
                body(c * 2 + 1, 1)
                body(c * 2 + 2, 0)
            body(PAIRS - 1, 1)
            after(PAIRS - 1)

        def x_loaded(t):
            return ld_x[t // R + 1 if t else 0], 16

        def cast_done(n):
            if n < FIRST_CASTS:
                return s_cast, 2 * ((FIRST_LOADS.index(n) if n < STAGES else n) + 1)
            return (s_cast, n + FIRST_CASTS + 1) if n % 2 == 0 else (s_cast_act, n - FIRST_CASTS + 2)

        def cast_of(n):
            src = stage[:, n % STAGES, :].rearrange("p (j w) -> p j w", j=JH)
            return adj[:, (n % 2) * JH:(n % 2 + 1) * JH, (n // 2) * LW:(n // 2 + 1) * LW], src

        at = bass.ds
        block = ctx.enter_context(nc.Block())

        @block.sync
        def _(sp):
            xr = x_in.rearrange("(t p) d -> p t d", p=P)
            sp.dma_start(x[:, 0, :], xr[:, 0, :]).then_inc(ld_x[0], 16)
            for r in range(R):
                first = max(r * R, 1)
                sp.dma_start(x[:, first:(r + 1) * R, :], xr[:, first:(r + 1) * R, :]).then_inc(ld_x[r + 1], 16)
            sp.dma_start(bias0, b0_in.rearrange("(a n) -> a n", a=1).partition_broadcast(P)).then_inc(ld_b, 16)
            adj_n = adj_in.rearrange("c h p w -> (c h) p w")

            def load_adj(n):
                if n >= STAGES:
                    sp.wait_ge(*cast_done(n - STAGES))
                sp.dma_start(stage[:, n % STAGES, :], adj_n[n]).then_inc(ld_adj[n % STAGES], 16)
            for n in FIRST_LOADS:
                load_adj(n)
            sp.dma_start(w1f, w1_in.rearrange("(k p) (h f) -> p k h f", p=P, h=H)).then_inc(ld_w1, 16)
            sp.dma_start(abc.rearrange("p h s f -> p (h s f)"),
                         a_in.rearrange("h f a -> a (h f)").partition_broadcast(P)).then_inc(ld_a, 16)
            load_adj(STAGES)
            load_adj(STAGES + 1)
            sp.dma_start(part(r_flat, (0, 4 * D), F32, "p (c f) -> p c f", c=4),
                         w2a_in.rearrange("(c p) f -> p c f", p=P)).then_inc(ld_w2a, 16)
            sp.dma_start(part(r_flat, (4 * D, 8 * D), F32, "p (c f) -> p c f", c=4),
                         w2b_in.rearrange("(c p) f -> p c f", p=P)).then_inc(ld_w2b, 16)
            sp.dma_start(w3f, w3_in.rearrange("(k p) f -> p k f", p=P)).then_inc(ld_w3, 16)
            for n in range(STAGES + 2, NL):
                load_adj(n)
            sp.wait_ge(s_ph, 2 * T)
            sp.dma_start(s_dram, srow).then_inc(s_srow, 16)
            sp.wait_ge(s_srow, 16)

            def load_rho(chunk, b):
                for hh in range(2):
                    sp.dma_start(rho[:, b, hh, :], s_dram[2 * b + hh:2 * b + hh + 1, at(chunk * CH, CH)]
                                 .partition_broadcast(P)).then_inc(ld_rho[b], 16)

            load_rho(0, 0)
            load_rho(0, 1)
            with sp.Fori(1, N // CH) as c:
                for b in range(2):
                    sp.wait_ge(s_a, c * (2 * T) + (b - 1) * T)
                    load_rho(c, b)

            def store(t, u):
                sp.wait_ge(s_norm, t + (3 * T + 1))
                sp.dma_start(out.rearrange("(t p) d -> t p d", p=P)[at(t, 1)].rearrange("a p d -> p (a d)"),
                             x[:, at(t, 1), :].rearrange("p a d -> p (a d)")).then_inc(s_out, 16)
            tiles(sp, 0, T, store)
            sp.wait_ge(s_out, 16 * T)

        LAST_BANKS = [*range(R, 2 * R), *range(R)]
        prep_w = {0: w0, 2: w2a, 3: w2b, 4: w3}

        def tile_of(buf, t):
            return buf[:, at(t, 1), :].rearrange("p a f -> p (a f)")

        @block.scalar
        def _(act):
            act.dma_start(w0f, w0_in.rearrange("(k p) h e -> p k (h e)", p=P)).then_inc(ld_w0, 16)

            def w0_hi():
                act.wait_ge(ld_w0, 16)
                nc.scalar.activation(w0[:, 0, :, :], w0f, ACT.Copy, scale=WS).then_inc(s_wh, 1)

            def split_hi(k, t, u, src, ready):
                ready(act)
                if not (k == 0 and isinstance(t, int) and t < R):
                    act.wait_ge(s_t, t + (k * T - R + 1))
                nc.scalar.activation(xs[:, u, 0, :], tile_of(src, t), ACT.Copy).then_inc(s_hi, 1)

            def take_t(k, t, u):
                act.wait_ge(s_t, t + (k * T + 1))
                nc.scalar.activation(tile_of(xt, t), tbank[u % 2], ACT.Copy).then_inc(s_xt, 1)

            def take_p(k, t, u):
                act.wait_ge(s_w, t + (k * T + 1))
                b = ps[:, 6 + u % 2, :]
                if k == 1:
                    nc.scalar.activation(srow[:, at(t * P, P)], b[0:H, P:2 * P], ACT.Copy, scale=1 / WS)\
                      .then_inc(s_ph, 1)
                    return
                dst = pset[k % 2][:, at(t, 1), 0, 0:D].rearrange("p a f -> p (a f)")
                src = b[:, D:2 * D] if k in (2, 3) else b[:, 0:D]
                if k == 4:
                    nc.scalar.activation(tile_of(own, t), src, ACT.Copy, scale=dis2w[:, at(t, 1)])
                nc.scalar.activation(dst, src, ACT.Copy, scale=disw[:, at(t, 1)] if k == 4 else 1 / WS)\
                  .then_inc(s_ph, 1)

            def joint(k, src, ready, between={}):
                for t in range(AHEAD):
                    split_hi(k, t, t, src, lambda e: ready(e, t))
                    if k == 0 and t == 0:
                        w0_hi()
                for t in range(1 + AHEAD - 1, T + AHEAD + 1):
                    if t < T:
                        split_hi(k, t, t % R, src, lambda e: ready(e, t))
                    if t - AHEAD < T:
                        take_t(k, t - AHEAD, (t - AHEAD) % R)
                    if t - AHEAD > 0:
                        take_p(k, t - AHEAD - 1, (t - AHEAD - 1) % R)
                    if t - AHEAD in between:
                        between[t - AHEAD]()

            def lagged(k, first=0):
                def one(t, u):
                    take_t(k, t, u)
                    take_p(k, t, u)
                tiles(act, first, T, one)

            def w1_hi(kk):
                act.wait_ge(ld_w1, 16)
                ins = nc.scalar.activation(w1[:, 0, kk, :], w1ff[:, kk, :], ACT.Copy, scale=WS)
                if kk == K2 - 1:
                    ins.then_inc(s_wh, 1)
            joint(0, x, lambda e, t: e.wait_ge(*x_loaded(t)), {11: lambda: w1_hi(0), 12: lambda: w1_hi(1)})
            act.wait_ge(s_w, T)
            for n, bi in enumerate((b1_in, b2_in)):
                act.dma_start(b12[:, n, :], bi.rearrange("(a n) -> a n", a=1).partition_broadcast(P)).then_inc(ld_b12, 16)

            def cast_n(n):
                act.wait_ge(ld_adj[n % STAGES], (n // STAGES + 1) * 16)
                nc.scalar.activation(*cast_of(n), ACT.Copy).then_inc(s_cast_act, 2)
            cast_n(FIRST_CASTS)
            for buf, src, s in ((w2a, w2af, ld_w2a), (w2b, w2bf, ld_w2b)):
                act.wait_ge(s, 16)
                nc.scalar.activation(buf[:, 0, :, :].rearrange("p k (s f) -> p k s f", s=2), src, ACT.Copy, scale=WS)\
                  .then_inc(s_wh, 1)

            act.wait_ge(ld_w3, 16)
            nc.scalar.activation(w3[:, 0, :, :], w3f, ACT.Copy, scale=WS).then_inc(s_wh, 1)
            act.wait_ge(s_wa, 4 * K2)
            nc.scalar.activation(was[:, 0], wa[:, :, :, :], ACT.Copy, scale=WS).then_inc(s_wah, 1)
            casts_after = {0: 7, 1: 9, 2: 11, 4: 13, 5: 15}
            for t in range(R + 2):
                take_t(1, t, t % R)
                if t == 0:
                    act.wait_ge(s_wl, 3)
                take_p(1, t, t % R)
                if t in casts_after:
                    cast_n(casts_after[t])
            lagged(1, R + 2)

            act.wait_ge(s_bias, 1)
            for h in range(H):
                nc.scalar.activation(bet[:, h, :], dall[:, :, h], ACT.Exp, scale=SLOPE, bias=bias_b[:, h:h + 1])\
                  .then_inc(s_gb, 1)

            def rho_exp(p, b):
                chunk16 = p // 2 if isinstance(p, int) else None
                act.wait_ge(ld_rho[b], 32 * (chunk16 + 1) if chunk16 is not None else (p + (2 - b)) * 16)
                if isinstance(p, int) and p < 2:
                    pass
                for hh in range(2):
                    h = 2 * b + hh
                    ins = nc.scalar.activation(rho[:, b, hh, :], rho[:, b, hh, :], ACT.Exp, scale=-(1 - SLOPE),
                                               bias=bias_g[:, h:h + 1])
                ins.then_inc(s_rx, 1)

            act.wait_ge(s_bw, 1)

            def value_hi(t, u):
                for half in range(2):
                    act.wait_ge(s_ht, t * 2 + (half + 1))
                    for hh in range(2):
                        h = 2 * half + hh
                        ins = nc.scalar.activation(
                            val[0][:, at(t, 1), h, 0:D].rearrange("p a f -> p (a f)"),
                            ps[:, 2 * u + half, hh * D:(hh + 1) * D], ACT.Copy, scale=betw[:, h, at(t, 1)])
                    ins.then_inc(s_yh, 1)
            tiles(act, 0, T - 2 * R, value_hi)
            act.wait_ge(s_bias, 2)
            for h in range(H):
                nc.scalar.activation(gam[:, h, :], dall[:, :, h], ACT.Exp, scale=1 - SLOPE, bias=bias_g[:, h:h + 1])\
                  .then_inc(s_gb, 1)
            rho_exp(0, 0)

            def exp_adj(p, q, jt):
                chunk = (p - q) // 2 if isinstance(p, int) else None
                n = p * T + jt
                if not isinstance(n, int) or n >= 2:
                    act.wait_ge(s_a, n - 1)
                col = chunk * CH if chunk is not None else (p - q) * (CH // 2)
                nc.scalar.activation(ring_e[:, jt % 2, :], adj[:, jt, at(col, CH)], ACT.Exp).then_inc(s_e, 1)

            def att_hi(p, jt):
                act.wait_ge(s_a, p * T + (jt + 1))
                if jt > 3:
                    act.wait_ge(s_mm, p * (T - 1) + (jt - 3))
                elif isinstance(p, int) and p == 0:
                    act.wait_ge(s_ht, 2 * R * (jt + 1))
                elif jt == 3:
                    act.wait_ge(s_z, p * (2 * R))
                else:
                    act.wait_ge(s_mm, p * (T - 1) + (jt - 2))
                nc.scalar.activation(ring_hl[:, jt % 4, 0], ring_a[:, jt % 2], ACT.Copy).then_inc(s_ah, 1)

            exp_adj(0, 0, 0)
            exp_adj(0, 0, 1)
            att_hi(0, 0)
            att_hi(0, 1)
            tiles(act, T - 2 * R, T, value_hi)

            def pair(p, q):
                for jt in range(T):
                    if isinstance(p, int) and p == 0 and jt < 2:
                        continue
                    exp_adj(p, q, jt)
                    if jt > 0 and not (isinstance(p, int) and p == 0 and jt == 2):
                        att_hi(p, jt - 1)
                    elif jt == 0:
                        att_hi(p - 1, T - 1)
                    if jt == 8 and not (isinstance(p, int) and p == PAIRS - 1):
                        rho_exp(p + 1, 1 - q)
            pairs(act, pair, lambda p: att_hi(p, T - 1))

            act.wait_ge(s_al[0], STEPS // 2)
            act.wait_ge(s_al[1], STEPS // 2)
            joint(2, x, lambda e, t: e.wait_ge(s_norm, t + (T + 1)))
            lagged(3)
            lagged(4)

        @block.tensor
        def _(pe):
            def transpose(k, t, u):
                pe.wait_ge(s_lo, t + (k * T + 1))
                if not (isinstance(t, int) and k == 0 and t < 2):
                    pe.wait_ge(s_xt, t + (k * T - 1))
                for c in range(2 * K2):
                    ins = nc.tensor.transpose(tbank[u % 2][:, c * P:(c + 1) * P],
                                              xs[:, u, c // K2, (c % K2) * P:(c % K2 + 1) * P], ident[:, :])
                ins.then_inc(s_t, 1)

            TERMS = [(0, 0), (0, 1), (1, 0)]

            def project(k, t, u):
                if k == 0 and isinstance(t, int) and t == 0:
                    pe.wait_ge(s_wl, 1)
                pe.wait_ge(s_xt, t + (k * T + 1))
                if not (isinstance(t, int) and k == 0 and t < 2):
                    pe.wait_ge(s_c, t + (k * T - 1))
                if k == 2 and isinstance(t, int) and t < 2:
                    pe.wait_ge(s_ev, 2 * R * (PAIRS - 1) + 3 + t)
                xtt = tile_of(xt, t)
                bank = ps[:, 6 + u % 2, :]

                def xpart(a, kk):
                    return xtt[:, (a * K2 + kk) * P:(a * K2 + kk + 1) * P]
                steps = [(a, b, kk) for kk in range(K2) for a, b in TERMS]
                if k == 1:
                    for n, (a, b, kk) in enumerate(steps):
                        nc.tensor.matmul(bank[:, 0:H], xpart(a, kk), was[:, b, kk, 1, :],
                                         start=(n == 0), stop=(n == len(steps) - 1))
                    for n, (a, b, kk) in enumerate(steps):
                        ins = nc.tensor.matmul(bank[0:H, P:2 * P], was[:, b, kk, 0, :], xpart(a, kk),
                                               start=(n == 0), stop=(n == len(steps) - 1))
                    ins.then_inc(s_w, 1)
                    return
                w = prep_w[k]
                width = w.shape[3]
                for n, (a, b, kk) in enumerate(steps):
                    ins = nc.tensor.matmul(bank[:, 0:width], xpart(a, kk), w[:, b, kk, :],
                                           start=(n == 0), stop=(n == len(steps) - 1))
                ins.then_inc(s_w, 1)

            def agg_step(a, k, it, bank, j, done):
                width = D + 1 if a == 0 else D
                pp = pset[k % 2]
                lhs = adj[:, j, at(it * P, P)]
                nc.tensor.matmul(ps[:, bank, 0:width], lhs, pp[:, j, 0, 0:width], start=(j == 0), stop=False)
                ins = nc.tensor.matmul(ps[:, bank, 0:D], lhs, pp[:, j, 1, 0:D], start=False, stop=(j == T - 1))
                if done:
                    ins.then_inc(s_acc, 1)

            def group0(a, k, js):
                if 0 in js and len(js) > 1:
                    order = [(j, it) for it in range(R) for j in js]
                else:
                    order = [(j, it) for j in js for it in range(R)]
                for n, (j, it) in enumerate(order):
                    if n < len(js) or it == 0:
                        pe.wait_ge(s_c, k * T + j + 1)
                    if j == 0 and a > 0:
                        pe.wait_ge(s_sum, (a - 1) * T + T - R + it + 1)
                    agg_step(a, k, it, it, j, j == T - 1)

            def joint(k, a, per, ready=lambda j: None):
                transpose(k, 0, 0)
                j = 0
                for t in range(T):
                    if t + 1 < T:
                        transpose(k, t + 1, (t + 1) % R)
                    project(k, t, t % R)
                    while j < per * (t + 1 - T) + T - 1:
                        ready(j)
                        group0(a, k, [j])
                        j += 1
                group0(a, k, [T - 1])

            def rest(a, knext, ready):
                k = (0, 2, 3, 4)[a]

                def one(t, u):
                    pe.wait_ge(s_sum, t + (a * T - R + 1))
                    prep = knext is not None and not (isinstance(t, int) and t == R)
                    for j in range(T):
                        if j % JH == 0:
                            ready(t, u, j // JH)
                        if j == T // 4 and prep:
                            transpose(knext, t - R - 1, (u - 1) % R)
                        if j == T // 2 + 2 and prep:
                            project(knext, t - R - 1, (u - 1) % R)
                        agg_step(a, k, t, u, j, j == T - 1)
                one(R, 0)
                tiles(pe, R + 1, T, one)

            def tail(k, a):
                e = T - R
                plan = [([], e - 1, None), ([0, 1, 2], e, e - 1), ([3, 4], e + 1, e), ([5, 6], e + 2, e + 1),
                        ([7, 8], e + 3, e + 2), ([9, 10], None, e + 3), (list(range(11, T)), None, None)]
                for js, tt, tp in plan:
                    group0(a, k, js)
                    if tt is not None:
                        transpose(k, tt, tt % R)
                    if tp is not None:
                        project(k, tp, tp % R)

            pe.wait_ge(s_id, 1)

            def columns_cast(j):
                if j == 0:
                    pe.wait_ge(s_one, 1)
                if j % JH == 0:
                    pe.wait_ge(*cast_done(STAGES // 2 + j // JH))
            joint(0, 0, 2, columns_cast)

            def cast_ready(t, u, half):
                if half == 0:
                    pe.wait_ge(s_cast, t + (FIRST_CASTS + 1 - u % 2))
                else:
                    pe.wait_ge(s_cast_act, t + (3 - FIRST_CASTS - u % 2))
                if isinstance(t, int) and t == R + 1:
                    pe.wait_ge(s_was, 1)
            rest(0, 1, cast_ready)

            def values_half(t, u, half):
                xtt = tile_of(xt, t)
                if not (isinstance(t, int) and t < R):
                    pe.wait_ge(s_yl, t * 2 + (half + 1 - 2 * R))
                steps = [(a, b, kk) for kk in range(K2) for a, b in TERMS]
                for n, (a, b, kk) in enumerate(steps):
                    ins = nc.tensor.matmul(ps[:, 2 * u + half, :], xtt[:, (a * K2 + kk) * P:(a * K2 + kk + 1) * P],
                                           w1[:, b, kk, half * 512:(half + 1) * 512],
                                           start=(n == 0), stop=(n == len(steps) - 1))
                ins.then_inc(s_ht, 1)

            def values(t, u):
                for half in range(2):
                    values_half(t, u, half)
            pe.wait_ge(s_wl, 5)
            transpose(1, T - R - 1, R - 1)
            transpose(1, T - R, 0)
            for n in range(R):
                pe.wait_ge(s_sum, T - R + n + 1)
                values_half(n // 2, n // 2, n % 2)
                project(1, T - R - 1 + n, (n - 1) % R)
                if n < R - 1:
                    transpose(1, T - R + n + 1, n + 1)
            pe.wait_ge(s_xt, 2 * T - 1)
            values_half(2, 2, 0)
            project(1, T - 1, R - 1)
            values_half(2, 2, 1)
            pe.wait_ge(s_c, 2 * T)
            values(3, 3)
            tiles(pe, R, T, values)

            pe.wait_ge(s_bl, 1)

            def pair(p, q):
                first = isinstance(p, int) and p == 0
                for jt in range(T):
                    pe.wait_ge(s_al[jt % 2], p * (T // 2) + (jt // 2 + 1))
                    for b in range(2 * R):
                        if isinstance(p, int) and p == PAIRS - 1 and jt == T - 1:
                            b = LAST_BANKS[b]
                        hh, it = b // R, b % R
                        if jt == 0 and first:
                            pe.wait_ge(s_yl, 2 * T - 2 * R + b + 1)
                        if jt == 0 and not first:
                            pe.wait_ge(s_ev, p * (2 * R) + (b + 1 - 2 * R))
                        h = 2 * q + hh
                        hi = ring_hl[:, jt % 4, 0, hh, it * P:(it + 1) * P]
                        lo = ring_hl[:, jt % 4, 1, hh, it * P:(it + 1) * P]
                        acc = ps[:, b, 0:D + 1]
                        nc.tensor.matmul(acc, hi, val[0][:, jt, h, 0:D + 1], start=(jt == 0), stop=False)
                        nc.tensor.matmul(acc, hi, val[1][:, jt, h, 0:D + 1], start=False, stop=False)
                        ins = nc.tensor.matmul(acc, lo, val[0][:, jt, h, 0:D + 1], start=False, stop=(jt == T - 1))
                        if jt == T - 1:
                            ins.then_inc(s_z, 1)
                    if jt < T - 1:
                        ins.then_inc(s_mm, 1)
            pairs(pe, pair, lambda p: None)

            pe.wait_ge(s_ev, 2 * R * (PAIRS - 1) + 2)

            def attention_read(j):
                if j == 0:
                    pe.wait_ge(s_ev, 2 * R * PAIRS)
            joint(2, 1, T // R, attention_read)
            rest(1, 3, lambda *_: None)
            tail(3, 2)
            rest(2, 4, lambda *_: None)
            tail(4, 3)
            rest(3, None, lambda *_: None)

        @block.vector
        def _(dve):
            def cast_n(n):
                dve.wait_ge(ld_adj[n % STAGES], (n // STAGES + 1) * 16)
                nc.vector.tensor_copy(*cast_of(n)).then_inc(s_cast, 2)

            def split_lo(k, t, u, src):
                dve.wait_ge(s_hi, t + (k * T + 1))
                nc.vector.tensor_sub(xs[:, u, 1, :], tile_of(src, t), xs[:, u, 0, :]).then_inc(s_lo, 1)

            def take(k, t, u):
                dve.wait_ge(s_ph, t + (k * T + 1))
                b = ps[:, 6 + u % 2, :]
                if k == 1:
                    nc.vector.tensor_scalar(tile_of(dall, t), b[:, 0:H], 1 / WS, None, ALU.mult).then_inc(s_c, 1)
                    return
                hi = pset[k % 2][:, at(t, 1), 0, 0:D].rearrange("p a f -> p (a f)")
                lo = pset[k % 2][:, at(t, 1), 1, 0:D].rearrange("p a f -> p (a f)")
                ot = tile_of(own, t)
                if k in (2, 3):
                    nc.vector.scalar_tensor_tensor(ot, b[:, 0:D], 1 / WS, b12[:, k - 2, :],
                                                   op0=ALU.mult, op1=ALU.add)
                src = b[:, D:2 * D] if k in (2, 3) else b[:, 0:D]
                nc.vector.scalar_tensor_tensor(lo, src, disw[:, at(t, 1)] if k == 4 else 1 / WS, hi,
                                               op0=ALU.mult, op1=ALU.subtract).then_inc(s_c, 1)

            def hold(s, value):
                dve.wait_ge(s, value)
                nc.vector.memset(held[:, :], 0.0)

            def statistics(l, slot):
                nc.vector.bn_stats(stat[:, slot, :], total[:, slot, :]).then_inc(s_stat, 1)
                hold(s_stat, l + 1)
                nc.vector.bn_aggr(mv[:, slot, :], stat[:, slot, :]).then_inc(s_aggr, 1)

            def normalise(l, slot, xt_):
                dve.wait_ge(s_rstd, l + 1)
                nc.vector.tensor_scalar(xt_, total[:, slot, :], mv[:, slot, 0:1], rstd[:, slot:slot + 1],
                                        ALU.subtract, ALU.mult).then_inc(s_norm, 1)

            def stages(a, k, t, u):
                q, l = t + a * T, t + (a - 2) * T
                acc, xt_, ot, ht_, tot = ps[:, u, 0:D], tile_of(x, t), tile_of(own, t), tile_of(hid, t), total[:, u, :]

                def first():
                    if a == 0 and isinstance(t, int) and t == 0:
                        dve.wait_ge(s_xb, T)
                    dve.wait_ge(s_acc, q + 1)
                    if a == 0:
                        nc.vector.tensor_copy(deg[:, at(t, 1)], ps[:, u, D:D + 1]).then_inc(s_deg, 1)
                        nc.vector.tensor_tensor(tot, acc, xt_, ALU.add).then_inc(s_sum, 1)
                    elif a == 3:
                        nc.vector.scalar_tensor_tensor(ot, acc, dis[:, at(t, 1)], ot, op0=ALU.mult, op1=ALU.add)\
                          .then_inc(s_sum, 1)
                    else:
                        nc.vector.tensor_tensor(ht_ if a == 1 else ot, acc, ot, ALU.add).then_inc(s_sum, 1)

                def relu():
                    dve.wait_ge(s_sum, q + 1)
                    if a == 1:
                        nc.vector.tensor_scalar(ht_, ht_, 0.0, None, ALU.max).then_inc(s_h, 1)
                    elif a == 2:
                        nc.vector.scalar_tensor_tensor(ot, ot, 0.0, ht_, op0=ALU.max, op1=ALU.add).then_inc(s_u, 1)

                def residual():
                    if a == 2:
                        dve.wait_ge(s_u, t + 1)
                    else:
                        dve.wait_ge(s_sum, q + 1)
                    nc.vector.scalar_tensor_tensor(tot, ot, 0.0, xt_, op0=ALU.max, op1=ALU.add).then_inc(s_v, 1)

                def stats():
                    if a == 0:
                        dve.wait_ge(s_sum, q + 1)
                    else:
                        dve.wait_ge(s_v, l + 1)
                    nc.vector.bn_stats(stat[:, u, :], tot).then_inc(s_stat, 1)

                def aggregate_stats():
                    hold(s_stat, q + 1)
                    nc.vector.bn_aggr(mv[:, u, :], stat[:, u, :]).then_inc(s_aggr, 1)

                out_ = [first]
                if a in (1, 2):
                    out_.append(relu)
                if a > 1:
                    out_.append(residual)
                if a != 1:
                    out_ += [stats, aggregate_stats]
                late_ = [lambda: normalise(q, u, xt_)] if a != 1 else []

                def split():
                    dve.wait_ge(s_t, t + (k * T - R + 1))
                    if a == 1:
                        dve.wait_ge(s_h, t + 1)
                        nc.vector.tensor_scalar(xs[:, u, 0, :], ht_, 0.0, None, ALU.max).then_inc(s_hi, 1)
                    else:
                        nc.vector.tensor_scalar(xs[:, u, 0, :], tot, mv[:, u, 0:1], rstd[:, u:u + 1],
                                                ALU.subtract, ALU.mult).then_inc(s_hi, 1)
                if k is not None:
                    late_.append(split)
                return out_, late_

            def first_sums(a, k):
                lines = [sum(stages(a, k, t, t), []) for t in range(R)]
                for s, st in enumerate(lines[0]):
                    st()
                    if 0 < s < R:
                        lines[s][0]()
                for line in lines[len(lines[0]):]:
                    line[0]()
                rows = len(lines[0])
                for s in range(1, rows + 1):
                    for t in (1, 2):
                        if 1 <= s - (t - 1) < rows:
                            lines[t][s - (t - 1)]()
                for n, st in enumerate(lines[3][1:]):
                    if n + 1 == len(lines[3]) - len(stages(a, k, 3, 3)[1]) and k is not None:
                        take(k, 0, 0)
                    st()

            def other_sums(a, k, fill={}):
                def one(t, u):
                    early, late_ = stages(a, k, t, u)[0], stages(a, k, t - 1, (u - 1) % R)[1]
                    if isinstance(t, int) and t == R:
                        late_ = []
                    if k is not None and not (isinstance(t, int) and t == R and a > 0):
                        late_.append(lambda: take(k, t - R, u))
                    if isinstance(t, int) and t in fill:
                        late_.append(fill[t])
                    for n in range(max(len(early), len(late_))):
                        for st in early[n:n + 1] + late_[n:n + 1]:
                            st()
                peeled = max(len(fill), 1)
                for t in range(R, R + peeled):
                    one(t, t % R)
                tiles(dve, R + peeled, T, one)
                for st in stages(a, k, T - 1, R - 1)[1]:
                    st()
                if k is not None:
                    for t in range(T - R, T):
                        take(k, t, t % R)

            def sum_products(n):
                dve.wait_ge(s_prod, n + 1)
                heads = slice(2 * (n % 2), 2 * (n % 2) + 2)
                nc.vector.reduce_sum(wa[:, n // 4, n // 2 % 2, heads], prod[:, heads], axis=AX.X).then_inc(s_wa, 1)

            CAST, SUM = cast_n, sum_products
            between = {5: [(CAST, 0)], 7: [(CAST, 2)], 9: [(CAST, 1)], 11: [(CAST, 3)], 12: [(SUM, 0)],
                       13: [(SUM, 1), (SUM, 2)], 14: [(SUM, 3), (CAST, 4), (SUM, 4)], 15: [(SUM, 5)],
                       16: [(SUM, 6)]}
            for t in range(T + AHEAD + 1):
                if t < T:
                    dve.wait_ge(*x_loaded(t))
                    split_lo(0, t, t % R, x)
                if t == 0:
                    dve.wait_ge(s_wh, 1)
                    nc.vector.scalar_tensor_tensor(w0[:, 1, :, :], w0f, WS, w0[:, 0, :, :],
                                                   op0=ALU.mult, op1=ALU.subtract).then_inc(s_wl, 1)
                if t > AHEAD:
                    take(0, t - AHEAD - 1, (t - AHEAD - 1) % R)
                for step, n in between.get(t - AHEAD, []):
                    step(n)

            def weight_lo(n, buf, src, halves=range(K2)):
                dve.wait_ge(s_wh, n + 1)
                for kk in halves:
                    hi, lo = buf[:, 0, kk, :], buf[:, 1, kk, :]
                    if n in (2, 3):
                        hi, lo = (v.rearrange("p (s f) -> p s f", s=2) for v in (hi, lo))
                    ins = nc.vector.scalar_tensor_tensor(lo, src[:, kk], WS, hi, op0=ALU.mult, op1=ALU.subtract)
                if kk == K2 - 1:
                    ins.then_inc(s_wl, 1)

            def was_lo():
                dve.wait_ge(s_wah, 1)
                nc.vector.scalar_tensor_tensor(was[:, 1], wa[:, :, :, :], WS, was[:, 0],
                                               op0=ALU.mult, op1=ALU.subtract).then_inc(s_was, 1)

            fill = {0: was_lo, 1: lambda: weight_lo(3, w2b, w2bf), 2: lambda: cast_n(8),
                    3: lambda: weight_lo(4, w3, w3f), 4: lambda: cast_n(10), 5: lambda: weight_lo(1, w1, w1ff),
                    6: lambda: cast_n(12), 7: lambda: cast_n(14)}
            lines = [stages(0, 1, t, t) for t in range(R)]
            for line in lines:
                line[0][0]()
            sum_products(7)
            for t, (early, late_) in enumerate(lines):
                for st in early[1:]:
                    st()
                fill[t]()
                for st in late_:
                    st()
                if t == 0:
                    cast_n(6)
                    weight_lo(2, w2a, w2af)
            other_sums(0, 1, {t: fill[t] for t in range(R, 2 * R)})

            dve.wait_ge(s_c, 2 * T)
            nc.vector.reduce_max(dmx[:, :], dall[:, :, :].rearrange("p t h -> p h t"), axis=AX.X).then_inc(s_dmx, 1)
            dve.wait_ge(s_dmb, 1)
            nc.vector.tensor_scalar(bias_b[:, :], dmb[:, :], -SLOPE, None, ALU.mult).then_inc(s_bias, 1)
            nc.vector.tensor_scalar(bias_g[:, :], dmb[:, :], -(1 - SLOPE), LCAP, ALU.mult, ALU.add).then_inc(s_bias, 1)
            dve.wait_ge(s_gb, H)
            nc.vector.tensor_scalar(betw[:, :, :], bet[:, :, :], 1 / WS, None, ALU.mult).then_inc(s_bw, 1)
            nc.vector.tensor_scalar(bet4[:, :, :], bet[:, :, :], float(H), None, ALU.mult).then_inc(s_bw, 1)
            dve.wait_ge(s_bw, 2)

            def value_lo(t, u):
                for half in range(2):
                    dve.wait_ge(s_yh, t * 2 + (half + 1))
                    for hh in range(2):
                        h = 2 * half + hh
                        ins = nc.vector.scalar_tensor_tensor(
                            val[1][:, at(t, 1), h, 0:D].rearrange("p a f -> p (a f)"),
                            ps[:, 2 * u + half, hh * D:(hh + 1) * D], betw[:, h, at(t, 1)],
                            val[0][:, at(t, 1), h, 0:D].rearrange("p a f -> p (a f)"),
                            op0=ALU.mult, op1=ALU.subtract)
                    ins.then_inc(s_yl, 1)
            value_lo(0, 0)
            b4 = bet4[:, :, :].rearrange("p h t -> p t h")
            nc.vector.tensor_copy(val[0][:, :, :, D], b4).then_inc(s_bh, 1)
            dve.wait_ge(s_bh, 1)
            nc.vector.tensor_tensor(val[1][:, :, :, D], b4, val[0][:, :, :, D], ALU.subtract).then_inc(s_bl, 1)
            for t in range(1, R):
                value_lo(t, t)
            tiles(dve, R, T - 2 * R, value_lo)
            dve.wait_ge(s_gb, 2 * H)

            def cap_rho(p, b):
                dve.wait_ge(s_rx, p + 1)
                nc.vector.tensor_scalar(rho[:, b], rho[:, b], math.exp(LCAP), None, ALU.min).then_inc(s_rho, 1)
            cap_rho(0, 0)

            def weights(p, q, jt):
                n = p * T + jt
                if jt == 0:
                    dve.wait_ge(s_rho, p + 1)
                dve.wait_ge(s_e, n + 1)
                if not isinstance(n, int) or n >= 2:
                    dve.wait_ge(s_ah, n - 1)
                    dve.wait_ge(s_al[jt % 2], p * (T // 2) + jt // 2)
                for hh in range(2):
                    h = 2 * q + hh
                    ins = nc.vector.scalar_tensor_tensor(
                        ring_a[:, jt % 2, hh, :], rho[:, q, hh, :], gam[:, h, jt:jt + 1], ring_e[:, jt % 2, :],
                        op0=ALU.max, op1=ALU.mult)
                ins.then_inc(s_a, 1)

            def att_lo(m, jt):
                dve.wait_ge(s_ah, m + 1)
                nc.vector.tensor_sub(ring_hl[:, jt % 4, 1], ring_a[:, jt % 2], ring_hl[:, jt % 4, 0])\
                  .then_inc(s_al[0], 1)

            weights(0, 0, 0)
            weights(0, 0, 1)
            att_lo(0, 0)
            tiles(dve, T - 2 * R, T, value_lo)

            def take_attention(p, q, banks=range(2 * R)):
                first = (p - q) * 2
                for n in range(2 * R + 1):
                    if n < 2 * R:
                        b = banks[n]
                        dve.wait_ge(s_z, p * (2 * R) + (n + 1))
                        nc.vector.reciprocal(rden[:, b:b + 1], ps[:, b, D:D + 1]).then_inc(s_rd, 1)
                    if n == 0:
                        continue
                    b, it = banks[n - 1], banks[n - 1] % R
                    dve.wait_ge(s_rd, p * (2 * R) + n)
                    if n > R:
                        dve.wait_ge(s_ev, p * (2 * R) + (it + 1))
                    xt_ = tile_of(x, first + it)
                    dst = total[:, it, :] if q == 1 and n > R else xt_
                    nc.vector.scalar_tensor_tensor(dst, ps[:, b, 0:D], rden[:, b:b + 1], xt_,
                                                   op0=ALU.mult, op1=ALU.add).then_inc(s_ev, 1)

            def chunk_statistics(p, its=range(R)):
                first = (p - 1) * 2
                for it in its:
                    dve.wait_ge(s_ev, p * (2 * R) + R + it + 1)
                    statistics(first + (T + it), it)

            def chunk_normalise(p, its=range(R)):
                first = (p - 1) * 2
                for it in its:
                    normalise(first + (T + it), it, tile_of(x, first + it))

            def pair(p, q):
                first = isinstance(p, int) and p == 0
                for jt in range(T):
                    if not (first and jt < 2):
                        weights(p, q, jt)
                        if jt % 2 == 1:
                            att_lo(p * T + (jt - 1), jt - 1)
                    if not first:
                        if jt == 2:
                            take_attention(p - 1, 1 - q)
                        if q == 0 and jt == 5:
                            chunk_statistics(p - 1)
                        if q == 0 and jt == 8:
                            chunk_normalise(p - 1)
                    if jt == 12 and not (isinstance(p, int) and p == PAIRS - 1):
                        cap_rho(p + 1, 1 - q)

            def end(p):
                for t in range(AHEAD):
                    split_lo(2, t, t, x)
                take_attention(p, 1, LAST_BANKS)
            pairs(dve, pair, end)

            NORMS_AT = T - R - 5
            dve.wait_ge(ld_b12, 32)
            for t in range(AHEAD, T + AHEAD + 1):
                if t < T:
                    split_lo(2, t, t % R, x)
                if 0 <= t - NORMS_AT < R:
                    chunk_statistics(PAIRS - 1, [t - NORMS_AT])
                if 0 < t - NORMS_AT <= R:
                    chunk_normalise(PAIRS - 1, [t - NORMS_AT - 1])
                if t > AHEAD:
                    take(2, t - AHEAD - 1, (t - AHEAD - 1) % R)
            first_sums(1, 3)
            other_sums(1, 3)
            first_sums(2, 4)
            other_sums(2, 4)
            first_sums(3, None)
            other_sums(3, None)

        @block.gpsimd
        def _(pool):
            nc.gpsimd.memset(ident[:, :], 0.0).then_inc(s_id0, 1)
            nc.gpsimd.memset(pset[0][:, :, 0, D:D + 1], 1.0).then_inc(s_one, 1)
            pool.wait_ge(s_id0, 1)
            nc.gpsimd.affine_select(out=ident[:, :], in_=ident[:, :], compare_op=ALU.not_equal, fill=1.0, base=0,
                                    pattern=[[-1, P]], channel_multiplier=1).then_inc(s_id, 1)
            nc.gpsimd.memset(neghalf[:, :], -0.5).then_inc(s_nh, 1)
            nc.gpsimd.memset(epsv[:, :], EPS).then_inc(s_nh, 1)
            pool.wait_ge(s_nh, 2)
            pool.wait_ge(ld_b, 16)

            def add_b0(t, u):
                pool.wait_ge(s_lo, t + 1)
                nc.gpsimd.tensor_tensor(tile_of(x, t), tile_of(x, t), bias0, ALU.add).then_inc(s_xb, 1)
            tiles(pool, 0, T, add_b0)
            pool.wait_ge(ld_w1, 16)
            pool.wait_ge(ld_a, 16)
            for n in range(4 * K2):
                heads = slice(2 * (n % 2), 2 * (n % 2) + 2)
                if n >= 2:
                    pool.wait_ge(s_wa, n - 1)
                nc.gpsimd.tensor_tensor(prod[:, heads], w1f[:, n // 4, heads], abc[:, heads, n // 2 % 2, :], ALU.mult)\
                  .then_inc(s_prod, 1)

            def inv_std(l, slot):
                pool.wait_ge(s_aggr, l + 1)
                nc.gpsimd.tensor_tensor(veps[:, slot:slot + 1], mv[:, slot, 1:2], epsv[:, :], ALU.add).then_inc(s_ve, 1)
                pool.wait_ge(s_ve, l + 1)
                nc.gpsimd.tensor_tensor(rstd[:, slot:slot + 1], veps[:, slot:slot + 1], neghalf[:, 0:1], ALU.pow)\
                  .then_inc(s_rstd, 1)

            def prep_lo(k, t, u, src):
                pool.wait_ge(s_hi, t + (k * T + 1))
                nc.gpsimd.tensor_sub(xs[:, u, 1, :], tile_of(src, t), xs[:, u, 0, :]).then_inc(s_lo, 1)

            def norm_and_lo(t, u):
                inv_std(t, u)
                prep_lo(1, t, u, x)
            tiles(pool, 0, T, norm_and_lo)
            pool.wait_ge(s_dmx, 1)
            nc.gpsimd.partition_all_reduce(dmb[:, :], dmx[:, :], P, bass.bass_isa.ReduceOp.max).then_inc(s_dmb, 1)
            pool.wait_ge(s_deg, T)
            nc.gpsimd.tensor_scalar(degp[:, :], deg[:, :], 1.0, None, ALU.add).then_inc(s_degp, 1)
            pool.wait_ge(s_degp, 1)
            nc.gpsimd.tensor_tensor(dis[:, :], degp[:, :], neghalf[:, :], ALU.pow).then_inc(s_dis, 1)
            pool.wait_ge(s_dis, 1)
            nc.gpsimd.tensor_scalar(disw[:, :], dis[:, :], 1 / WS, None, ALU.mult).then_inc(s_disw, 1)
            pool.wait_ge(s_disw, 1)
            nc.gpsimd.tensor_tensor(dis2w[:, :], disw[:, :], dis[:, :], ALU.mult).then_inc(s_disw, 1)

            def att_lo(m, jt):
                pool.wait_ge(s_ah, m + 1)
                nc.gpsimd.tensor_sub(ring_hl[:, jt % 4, 1], ring_a[:, jt % 2], ring_hl[:, jt % 4, 0])\
                  .then_inc(s_al[1], 1)

            def pair(p, q):
                first = isinstance(p, int) and p == 0
                for jt in range(1, T, 2):
                    att_lo(p * T + jt, jt)
                    if jt == 5 and q == 0 and not first:
                        for it in range(R):
                            inv_std((p - 2) * 2 + (T + it), it)
            pairs(pool, pair, lambda p: [inv_std((p - 1) * 2 + (T + it), it) for it in range(R)])
            tiles(pool, 0, T, lambda t, u: prep_lo(3, t, u, hid))

            def norm_and_last_lo(t, u):
                inv_std(t + 2 * T, u)
                prep_lo(4, t, u, x)
            tiles(pool, 0, T, norm_and_last_lo)
            tiles(pool, 3 * T, 4 * T, inv_std)


_ORDER = ["x", "adj", "L0_gnn_W", "L0_gnn_b", "L1_gnn_W", "L1_gnn_a", "L2_gnn_W1", "L2_gnn_b1", "L2_gnn_W2",
          "L2_gnn_b2", "L3_gnn_W"]


def kernel(**inputs):
    import numpy as np
    import concourse.bacc as bacc
    from concourse import mybir as _mybir
    from concourse.bass_utils import run_bass_kernel_spmd

    host = {k: np.asarray(inputs[k]) for k in _ORDER}
    n = host["adj"].shape[0]
    blocks, halves, p = 8, 2, 128
    host["adj"] = np.ascontiguousarray(
        host["adj"].T.reshape(halves, n // (halves * p), p, blocks, n // blocks).transpose(3, 0, 2, 1, 4)
        .reshape(blocks, halves, p, -1))
    host["L0_gnn_W"] = np.ascontiguousarray(host["L0_gnn_W"].transpose(1, 0, 2))
    host["L0_gnn_b"] = host["L0_gnn_b"].reshape(-1)

    nc = bacc.Bacc("TRN2", target_bir_lowering=False, num_devices=1)
    arrays, args = {}, []
    for k in _ORDER:
        a = np.ascontiguousarray(host[k])
        arrays[f"in_{k}"] = a
        args.append(nc.dram_tensor(f"in_{k}", a.shape, _mybir.dt.from_np(a.dtype), kind="ExternalInput").ap())
    args.append(nc.dram_tensor("out_x", host["x"].shape, _mybir.dt.float32, kind="ExternalOutput").ap())
    graph_stack(nc, *args)
    r = run_bass_kernel_spmd(nc, [arrays], core_ids=[0])
    return r.results[0]["out_x"]
```
